# Optimizing a Trainium2 kernel written in Bass

```python
import numpy as np
import jax
import jax.numpy as jnp

def _softmax(x, axis=-1):
    return jax.nn.softmax(x, axis=axis)

def _gelu(x):
    return jax.nn.gelu(x, approximate=True)

def _silu(x):
    return jax.nn.silu(x)

def _sigmoid(x):
    return jax.nn.sigmoid(x)

def _layernorm(x, axis=-1, eps=1e-05):
    m = jnp.mean(x, axis=axis, keepdims=True)
    v = jnp.var(x, axis=axis, keepdims=True)
    return (x - m) / jnp.sqrt(v + eps)

def _scatter_add(tgt, idx, src, axis=0):
    return tgt.at[idx].add(src)

def _segment_sum(src, seg, n):
    return jax.ops.segment_sum(src, seg, n)
kernel_name = 'mk_xattn_ffn_d2_seqx_r4_3b6046'

def setup_inputs(seed: int=0):
    np.random.seed(seed)
    _w = jnp.asarray

    def _rec_inputs():
        import jax
        import jax.numpy as jnp
        _rk = jax.random.key(seed)
        x = -0.0002928 + 1 * jax.random.normal(jax.random.fold_in(_rk, 1), (8, 256, 256), jnp.float32)
        _lenS = 256 - jax.random.randint(jax.random.fold_in(_rk, 7), (8,), 0, max(1, 256 // 4) + 1, jnp.int32)
        _lenS2 = 77 - jax.random.randint(jax.random.fold_in(_rk, 8), (8,), 0, max(1, 77 // 4) + 1, jnp.int32)
        _ctx_1024P = jax.random.normal(jax.random.fold_in(_rk, 11), (8, 16, 256), jnp.float32)
        _ctx_1024c = jax.random.dirichlet(jax.random.fold_in(_rk, 511), 0.3 * jnp.ones((16,), jnp.float32), (8, 77))
        _ctx_1024t = jnp.einsum('bsk,bkd->bsd', _ctx_1024c, _ctx_1024P)
        _ctx_1024t = _ctx_1024t * jax.lax.rsqrt(jnp.mean(jnp.square(_ctx_1024t)) + 1e-12) * 0.953939
        ctx_1024 = 4.13588e-05 + 0.999923 * (_ctx_1024t + 0.3 * jax.random.normal(jax.random.fold_in(_rk, 611), (8, 77, 256), jnp.float32))
        _validS = jnp.arange(256)[None, :] < _lenS[:, None]
        _validS2 = jnp.arange(77)[None, :] < _lenS2[:, None]
        _causal = jnp.tril(jnp.ones((256, 256), dtype=bool))
        mask_Bx1x1xS2_ff0 = jnp.where(jnp.ones((8, 1, 1, 77), dtype=bool), 0.0, -1000000000.0).astype(jnp.float32)
        mask_SxS2_bk1 = jnp.broadcast_to(_validS2[0:1, :], (256, 77))
        return (x, ctx_1024, mask_Bx1x1xS2_ff0, mask_SxS2_bk1)
    x, ctx_1024, mask_Bx1x1xS2_ff0, mask_SxS2_bk1 = _rec_inputs()

    def _L0_xattn_setup():
        import jax, jax.numpy as jnp
        import numpy as np
        H = 16
        D = 256
        F = 1024
        LN_EPS = 1e-05

        def _glorot(key, shape):
            fan_in, fan_out = (shape[0], shape[1])
            lim = np.sqrt(6.0 / (fan_in + fan_out))
            return jax.random.uniform(key, shape, jnp.float32, -lim, lim)

        def _split_heads(x):
            b, l, _ = x.shape
            return x.reshape(b, l, H, D // H)

        def _mha(x, ctx, mask, qw, qb, kw, kb, vw, vb):
            q = _split_heads(x @ qw + qb)
            k = _split_heads(ctx @ kw + kb)
            v = _split_heads(ctx @ vw + vb)
            scores = jnp.einsum('bqhd,bkhd->bhqk', q, k) / np.sqrt(D // H).astype(np.float32)
            if mask is not None:
                scores = scores + mask
            probs = jax.nn.softmax(scores, axis=-1)
            out = jnp.einsum('bhqk,bkhd->bqhd', probs, v)
            return out.reshape(x.shape[0], x.shape[1], D)

        def _self_output(h, residual, w, b, g, be):
            h = h @ w + b
            h = h + residual
            mu = jnp.mean(h, axis=-1, keepdims=True)
            var = jnp.mean(jnp.square(h - mu), axis=-1, keepdims=True)
            return (h - mu) * jax.lax.rsqrt(var + LN_EPS) * g + be
        key = jax.random.key(seed)
        ks = jax.random.split(key, 16)
        inp = {'input_tensor': jax.random.normal(ks[0], (4, 256, D), jnp.float32), 'ctx_tensor': jax.random.normal(ks[1], (4, 512, D), jnp.float32), 'ctx_attn_mask': jnp.zeros((4, 1, 1, 512), jnp.float32), 'cq_w': _glorot(ks[2], (D, D)), 'cq_b': jnp.zeros((D,)), 'ck_w': _glorot(ks[3], (D, D)), 'ck_b': jnp.zeros((D,)), 'cv_w': _glorot(ks[4], (D, D)), 'cv_b': jnp.zeros((D,)), 'co_w': _glorot(ks[5], (D, D)), 'co_b': jnp.zeros((D,)), 'co_g': jnp.ones((D,)), 'co_be': jnp.zeros((D,)), 'sq_w': _glorot(ks[6], (D, D)), 'sq_b': jnp.zeros((D,)), 'sk_w': _glorot(ks[7], (D, D)), 'sk_b': jnp.zeros((D,)), 'sv_w': _glorot(ks[8], (D, D)), 'sv_b': jnp.zeros((D,)), 'so_w': _glorot(ks[9], (D, D)), 'so_b': jnp.zeros((D,)), 'so_g': jnp.ones((D,)), 'so_be': jnp.zeros((D,)), 'fi_w': _glorot(ks[10], (D, F)), 'fi_b': jnp.zeros((F,)), 'fo_w': _glorot(ks[11], (F, D)), 'fo_b': jnp.zeros((D,)), 'fo_g': jnp.ones((D,)), 'fo_be': jnp.zeros((D,))}
        return inp
    _L0_xattn_all = _L0_xattn_setup()
    _L0_xattn_in = {k: v for k, v in _L0_xattn_all.items() if k in ('cq_w', 'cq_b', 'ck_w', 'ck_b', 'cv_w', 'cv_b', 'co_w', 'co_b', 'co_g', 'co_be', 'sq_w', 'sq_b', 'sk_w', 'sk_b', 'sv_w', 'sv_b', 'so_w', 'so_b', 'so_g', 'so_be', 'fi_w', 'fi_b', 'fo_w', 'fo_b', 'fo_g', 'fo_be')}
    del _L0_xattn_all

    def _L0_ffn_setup():
        import jax, jax.numpy as jnp
        import numpy as np
        FP8_MAX = 448.0
        SCALE = 1.0
        _FP8_DTYPE = getattr(jnp, 'float8_e4m3fn', jnp.float16)

        def quantize_e4m3(t, scale):
            return jnp.clip(t / scale, -FP8_MAX, FP8_MAX).astype(_FP8_DTYPE)
        key = jax.random.key(seed)
        kx, kw = jax.random.split(key)
        B, N, C, F = (8, 1024, 256, 256)
        x = jax.random.normal(kx, (B, N, C), dtype=jnp.float32)
        weight = jax.random.normal(kw, (F, C), dtype=jnp.float32) * 0.02
        bias = jnp.zeros((F,), dtype=jnp.float32)
        return {'x': x, 'weight': weight, 'bias': bias}
    _L0_ffn_all = _L0_ffn_setup()
    _L0_ffn_in = {k: v for k, v in _L0_ffn_all.items() if k in ('weight', 'bias')}
    del _L0_ffn_all

    def _L1_xattn_setup():
        import jax, jax.numpy as jnp
        import numpy as np
        D = 256
        H = 16
        HD = D // H
        SCALE = 1.0 / np.sqrt(HD)

        def _split_heads(x):
            B, S, _ = x.shape
            return x.reshape(B, S, H, HD).transpose(0, 2, 1, 3)
        key = jax.random.key(seed)
        ks = jax.random.split(key, 12)
        B, S = (4, 512)
        inp = {'queries': jax.random.normal(ks[0], (B, S, D), jnp.float32), 'keys': jax.random.normal(ks[1], (B, S, D), jnp.float32), 'values': jax.random.normal(ks[2], (B, S, D), jnp.float32), 'mask': jax.random.randint(ks[3], (S, S), 0, 2).astype(bool), 'Wq': jax.random.normal(ks[4], (D, D), jnp.float32) * 0.02, 'bq': jax.random.normal(ks[5], (D,), jnp.float32) * 0.02, 'Wk': jax.random.normal(ks[6], (D, D), jnp.float32) * 0.02, 'bk': jax.random.normal(ks[7], (D,), jnp.float32) * 0.02, 'Wv': jax.random.normal(ks[8], (D, D), jnp.float32) * 0.02, 'bv': jax.random.normal(ks[9], (D,), jnp.float32) * 0.02, 'Wo': jax.random.normal(ks[10], (D, D), jnp.float32) * 0.02, 'bo': jax.random.normal(ks[11], (D,), jnp.float32) * 0.02}
        return inp
    _L1_xattn_all = _L1_xattn_setup()
    _L1_xattn_in = {k: v for k, v in _L1_xattn_all.items() if k in ('Wq', 'bq', 'Wk', 'bk', 'Wv', 'bv', 'Wo', 'bo')}
    del _L1_xattn_all

    def _L1_ffn_setup():
        import jax, jax.numpy as jnp
        import numpy as np
        IN_F = 256
        OUT_F = 256
        N_EXPERTS = 8
        TOP_K = 2
        key = jax.random.key(seed)
        ks = jax.random.split(key, 5)
        scale_in = 1.0 / np.sqrt(IN_F)
        x = jax.random.normal(ks[0], (4, 512, IN_F), dtype=jnp.float32)
        W_experts = jax.random.uniform(ks[1], (N_EXPERTS, OUT_F, IN_F), jnp.float32, -scale_in, scale_in)
        b_experts = jax.random.uniform(ks[2], (N_EXPERTS, OUT_F), jnp.float32, -scale_in, scale_in)
        W_router = jax.random.uniform(ks[3], (N_EXPERTS, IN_F), jnp.float32, -scale_in, scale_in)
        b_router = jax.random.uniform(ks[4], (N_EXPERTS,), jnp.float32, -scale_in, scale_in)
        return {'x': x, 'W_experts': W_experts, 'b_experts': b_experts, 'W_router': W_router, 'b_router': b_router}
    _L1_ffn_all = _L1_ffn_setup()
    _L1_ffn_in = {k: v for k, v in _L1_ffn_all.items() if k in ('W_experts', 'b_experts', 'W_router', 'b_router')}
    del _L1_ffn_all
    return {'x': x, 'ctx_1024': ctx_1024, 'mask_Bx1x1xS2_ff0': mask_Bx1x1xS2_ff0, 'mask_SxS2_bk1': mask_SxS2_bk1, 'L0_xattn_cq_w': _L0_xattn_in['cq_w'], 'L0_xattn_cq_b': _L0_xattn_in['cq_b'], 'L0_xattn_ck_w': _L0_xattn_in['ck_w'], 'L0_xattn_ck_b': _L0_xattn_in['ck_b'], 'L0_xattn_cv_w': _L0_xattn_in['cv_w'], 'L0_xattn_cv_b': _L0_xattn_in['cv_b'], 'L0_xattn_co_w': _L0_xattn_in['co_w'], 'L0_xattn_co_b': _L0_xattn_in['co_b'], 'L0_xattn_co_g': _L0_xattn_in['co_g'], 'L0_xattn_co_be': _L0_xattn_in['co_be'], 'L0_xattn_sq_w': _L0_xattn_in['sq_w'], 'L0_xattn_sq_b': _L0_xattn_in['sq_b'], 'L0_xattn_sk_w': _L0_xattn_in['sk_w'], 'L0_xattn_sk_b': _L0_xattn_in['sk_b'], 'L0_xattn_sv_w': _L0_xattn_in['sv_w'], 'L0_xattn_sv_b': _L0_xattn_in['sv_b'], 'L0_xattn_so_w': _L0_xattn_in['so_w'], 'L0_xattn_so_b': _L0_xattn_in['so_b'], 'L0_xattn_so_g': _L0_xattn_in['so_g'], 'L0_xattn_so_be': _L0_xattn_in['so_be'], 'L0_xattn_fi_w': _L0_xattn_in['fi_w'], 'L0_xattn_fi_b': _L0_xattn_in['fi_b'], 'L0_xattn_fo_w': _L0_xattn_in['fo_w'], 'L0_xattn_fo_b': _L0_xattn_in['fo_b'], 'L0_xattn_fo_g': _L0_xattn_in['fo_g'], 'L0_xattn_fo_be': _L0_xattn_in['fo_be'], 'L0_ffn_weight': _L0_ffn_in['weight'], 'L0_ffn_bias': _L0_ffn_in['bias'], 'L1_xattn_Wq': _L1_xattn_in['Wq'], 'L1_xattn_bq': _L1_xattn_in['bq'], 'L1_xattn_Wk': _L1_xattn_in['Wk'], 'L1_xattn_bk': _L1_xattn_in['bk'], 'L1_xattn_Wv': _L1_xattn_in['Wv'], 'L1_xattn_bv': _L1_xattn_in['bv'], 'L1_xattn_Wo': _L1_xattn_in['Wo'], 'L1_xattn_bo': _L1_xattn_in['bo'], 'L1_ffn_W_experts': _L1_ffn_in['W_experts'], 'L1_ffn_b_experts': _L1_ffn_in['b_experts'], 'L1_ffn_W_router': _L1_ffn_in['W_router'], 'L1_ffn_b_router': _L1_ffn_in['b_router']}

def reference(x, ctx_1024, mask_Bx1x1xS2_ff0, mask_SxS2_bk1, L0_xattn_cq_w, L0_xattn_cq_b, L0_xattn_ck_w, L0_xattn_ck_b, L0_xattn_cv_w, L0_xattn_cv_b, L0_xattn_co_w, L0_xattn_co_b, L0_xattn_co_g, L0_xattn_co_be, L0_xattn_sq_w, L0_xattn_sq_b, L0_xattn_sk_w, L0_xattn_sk_b, L0_xattn_sv_w, L0_xattn_sv_b, L0_xattn_so_w, L0_xattn_so_b, L0_xattn_so_g, L0_xattn_so_be, L0_xattn_fi_w, L0_xattn_fi_b, L0_xattn_fo_w, L0_xattn_fo_b, L0_xattn_fo_g, L0_xattn_fo_be, L0_ffn_weight, L0_ffn_bias, L1_xattn_Wq, L1_xattn_bq, L1_xattn_Wk, L1_xattn_bk, L1_xattn_Wv, L1_xattn_bv, L1_xattn_Wo, L1_xattn_bo, L1_ffn_W_experts, L1_ffn_b_experts, L1_ffn_W_router, L1_ffn_b_router):
    import jax
    import jax.numpy as jnp

    def _L0_xattn_ref(input_tensor, ctx_tensor, ctx_attn_mask, cq_w, cq_b, ck_w, ck_b, cv_w, cv_b, co_w, co_b, co_g, co_be, sq_w, sq_b, sk_w, sk_b, sv_w, sv_b, so_w, so_b, so_g, so_be, fi_w, fi_b, fo_w, fo_b, fo_g, fo_be):
        import jax, jax.numpy as jnp
        import numpy as np
        H = 16
        D = 256
        F = 1024
        LN_EPS = 1e-05

        def _glorot(key, shape):
            fan_in, fan_out = (shape[0], shape[1])
            lim = np.sqrt(6.0 / (fan_in + fan_out))
            return jax.random.uniform(key, shape, jnp.float32, -lim, lim)

        def _split_heads(x):
            b, l, _ = x.shape
            return x.reshape(b, l, H, D // H)

        def _mha(x, ctx, mask, qw, qb, kw, kb, vw, vb):
            q = _split_heads(x @ qw + qb)
            k = _split_heads(ctx @ kw + kb)
            v = _split_heads(ctx @ vw + vb)
            scores = jnp.einsum('bqhd,bkhd->bhqk', q, k) / np.sqrt(D // H).astype(np.float32)
            if mask is not None:
                scores = scores + mask
            probs = jax.nn.softmax(scores, axis=-1)
            out = jnp.einsum('bhqk,bkhd->bqhd', probs, v)
            return out.reshape(x.shape[0], x.shape[1], D)

        def _self_output(h, residual, w, b, g, be):
            h = h @ w + b
            h = h + residual
            mu = jnp.mean(h, axis=-1, keepdims=True)
            var = jnp.mean(jnp.square(h - mu), axis=-1, keepdims=True)
            return (h - mu) * jax.lax.rsqrt(var + LN_EPS) * g + be
        ca = _mha(input_tensor, ctx_tensor, ctx_attn_mask, cq_w, cq_b, ck_w, ck_b, cv_w, cv_b)
        x = _self_output(ca, input_tensor, co_w, co_b, co_g, co_be)
        sa = _mha(x, x, None, sq_w, sq_b, sk_w, sk_b, sv_w, sv_b)
        x = _self_output(sa, x, so_w, so_b, so_g, so_be)
        inter = jax.nn.gelu(x @ fi_w + fi_b, approximate=False)
        x = _self_output(inter, x, fo_w, fo_b, fo_g, fo_be)
        return x

    def _L0_ffn_ref(x, weight, bias):
        import jax, jax.numpy as jnp
        import numpy as np
        FP8_MAX = 448.0
        SCALE = 1.0
        _FP8_DTYPE = getattr(jnp, 'float8_e4m3fn', jnp.float16)

        def quantize_e4m3(t, scale):
            return jnp.clip(t / scale, -FP8_MAX, FP8_MAX).astype(_FP8_DTYPE)
        B, N, C = x.shape
        x2d = x.reshape(B * N, C)
        x_mat = quantize_e4m3(x2d, SCALE).astype(jnp.float16)
        w_mat = quantize_e4m3(weight, SCALE).astype(jnp.float16)
        out2d = (x_mat @ w_mat.T).astype(jnp.float32) * (SCALE * SCALE)
        out2d = out2d + bias
        return out2d.reshape(B, N, -1)

    def _L1_xattn_ref(queries, keys, values, mask, Wq, bq, Wk, bk, Wv, bv, Wo, bo):
        import jax, jax.numpy as jnp
        import numpy as np
        D = 256
        H = 16
        HD = D // H
        SCALE = 1.0 / np.sqrt(HD)

        def _split_heads(x):
            B, S, _ = x.shape
            return x.reshape(B, S, H, HD).transpose(0, 2, 1, 3)
        q = _split_heads(queries @ Wq + bq)
        k = _split_heads(keys @ Wk + bk)
        v = _split_heads(values @ Wv + bv)
        scores = jnp.einsum('bhqd,bhkd->bhqk', q, k) * SCALE
        neg = jnp.finfo(scores.dtype).min
        scores = jnp.where(mask[None, None, :, :], scores, neg)
        probs = jax.nn.softmax(scores, axis=-1)
        ctx = jnp.einsum('bhqk,bhkd->bhqd', probs, v)
        B, _, Sq, _ = ctx.shape
        combined = ctx.transpose(0, 2, 1, 3).reshape(B, Sq, D)
        return combined @ Wo + bo

    def _L1_ffn_ref(x, W_experts, b_experts, W_router, b_router):
        import jax, jax.numpy as jnp
        import numpy as np
        IN_F = 256
        OUT_F = 256
        N_EXPERTS = 8
        TOP_K = 2
        router_logits = jnp.einsum('bsd,ed->bse', x, W_router) + b_router
        router_weights = jax.nn.softmax(router_logits, axis=-1)
        if TOP_K < N_EXPERTS:
            topk_w, topk_idx = jax.lax.top_k(router_weights, TOP_K)
            sparse = jnp.zeros_like(router_weights)
            router_weights = jnp.take_along_axis(sparse, topk_idx, axis=-1)
            router_weights = sparse.at[..., :].set(0.0)
            b_idx = jnp.arange(sparse.shape[0])[:, None, None]
            s_idx = jnp.arange(sparse.shape[1])[None, :, None]
            router_weights = sparse.at[b_idx, s_idx, topk_idx].set(topk_w)
        expert_out = jnp.einsum('bsd,eod->bseo', x, W_experts) + b_experts
        return jnp.einsum('bseo,bse->bso', expert_out, router_weights)
    x = x + _L0_xattn_ref(_layernorm(x, axis=-1), ctx_1024, mask_Bx1x1xS2_ff0, L0_xattn_cq_w, L0_xattn_cq_b, L0_xattn_ck_w, L0_xattn_ck_b, L0_xattn_cv_w, L0_xattn_cv_b, L0_xattn_co_w, L0_xattn_co_b, L0_xattn_co_g, L0_xattn_co_be, L0_xattn_sq_w, L0_xattn_sq_b, L0_xattn_sk_w, L0_xattn_sk_b, L0_xattn_sv_w, L0_xattn_sv_b, L0_xattn_so_w, L0_xattn_so_b, L0_xattn_so_g, L0_xattn_so_be, L0_xattn_fi_w, L0_xattn_fi_b, L0_xattn_fo_w, L0_xattn_fo_b, L0_xattn_fo_g, L0_xattn_fo_be)
    x = x + _L0_ffn_ref(_layernorm(x, axis=-1), L0_ffn_weight, L0_ffn_bias)
    x = x + _L1_xattn_ref(_layernorm(x, axis=-1), ctx_1024, ctx_1024, mask_SxS2_bk1, L1_xattn_Wq, L1_xattn_bq, L1_xattn_Wk, L1_xattn_bk, L1_xattn_Wv, L1_xattn_bv, L1_xattn_Wo, L1_xattn_bo)
    x = x + _L1_ffn_ref(_layernorm(x, axis=-1), L1_ffn_W_experts, L1_ffn_b_experts, L1_ffn_W_router, L1_ffn_b_router)
    return x

_drawn_inputs = setup_inputs


def setup_inputs(seed=0):
    import zlib

    import numpy as np

    out = dict(_drawn_inputs(seed))
    spreads = {'L0_xattn_cq_b': (0.0, 0.441),
     'L0_xattn_ck_b': (0.0, 2.0),
     'L0_xattn_cv_b': (0.0, 0.1),
     'L0_xattn_co_b': (0.0, 0.1),
     'L0_xattn_co_g': (1.0, 0.2),
     'L0_xattn_co_be': (0.0, 0.1),
     'L0_xattn_sq_b': (0.0, 0.8),
     'L0_xattn_sk_b': (0.0, 2.0),
     'L0_xattn_sv_b': (0.0, 0.1),
     'L0_xattn_so_b': (0.0, 0.1),
     'L0_xattn_so_g': (1.0, 0.2),
     'L0_xattn_so_be': (0.0, 0.1),
     'L0_xattn_fi_b': (0.0, 0.1),
     'L0_xattn_fo_b': (0.0, 0.1),
     'L0_xattn_fo_g': (1.0, 0.2),
     'L0_xattn_fo_be': (0.0, 0.1),
     'L0_ffn_bias': (0.0, 0.1)}
    factors = {'L1_xattn_Wq': 8.0,
     'L1_xattn_bq': 58.093,
     'L1_xattn_Wk': 8.0,
     'L1_xattn_bk': 64.0,
     'L1_xattn_bv': 8.0,
     'L1_xattn_bo': 4.28,
     'L1_ffn_b_experts': 8.0,
     'L1_ffn_b_router': 2.718}
    for name, (base, spread) in spreads.items():
        noise = np.random.default_rng([zlib.crc32(name.encode()), seed]).standard_normal(out[name].shape)
        drawn = base * np.exp(spread * noise) if base else spread * noise
        out[name] = jnp.asarray(drawn.astype(out[name].dtype))
    for name, factor in factors.items():
        out[name] = (out[name] * factor).astype(out[name].dtype)
    return out
```

```python
from contextlib import ExitStack

import numpy as np

import concourse.bass as bass
from concourse import mybir

ALU = mybir.AluOpType
ACT = mybir.ActivationFunctionType
AX = mybir.AxisListType
F32 = mybir.dt.float32
F32R = mybir.dt.float32r
FP16 = mybir.dt.float16
FP8 = mybir.dt.float8e4
U8 = mybir.dt.uint8
I32 = mybir.dt.int32

P = 128
B, S, D = 8, 256, 256
NK = 77
NKP = 78
MASK_WORDS = -(-NK // 4)
H, HD = 16, 16
F = 1024
NE = 8
TT = S // P
KC = D // P
HC = H // KC
NHP = HC // 2
STREAMS = 2
ITERS = B // STREAMS
EPS = 1e-5
NEG = -3.0e38
QSCALE = 1.0 / float(np.sqrt(HD))
FP8_MAX = 448.0

ROW_MAX = 3 * HD

CQ, CK, CV, CO, SQ, SK, SV, SO, LQ, LK, LV, LO = range(12)
FI, FO, EX = 12, 16, 20
NB = EX + NE
WEIGHTS_STEP = 2

B_CQ, B_CK, B_CV, B_SQ, B_SK, B_SV, B_LQ, B_LK, B_LV, G_CO, E_CO, G_SO, E_SO = range(0, 26, 2)
B_FI = 26
NCOL = B_FI + F // P

R_COB, R_G1, R_E1, R_G2, R_E2, R_G3, R_E3, R_FFB, R_LOB = range(9)
NROW = 9

ATT = [
    dict(q=CQ, k=CK, v=CV, o=CO, bq=B_CQ, bk=B_CK, bv=B_CV, ctx=True, kt=1),
    dict(q=SQ, k=SK, v=SV, o=SO, bq=B_SQ, bk=B_SK, bv=B_SV, ctx=False, kt=2),
    dict(q=LQ, k=LK, v=LV, o=LO, bq=B_LQ, bk=B_LK, bv=B_LV, ctx=True, kt=1),
]


def attention_phases(a):
    ctx = ATT[a]["ctx"]
    out = [("vproj", a)]
    for c in range(KC):
        out.append(("qk", a, c))
        out += [("ks", a, c, i) for i in range(1 if ctx else 2)]
        out += [("qs", a, c, i) for i in range(2)]
        out += [("mx", a, c, u) for u in range(4 if ctx else HC)]
        out.append(("mt", a, c))
        out += [("mq", a, c, i) for i in range(2)]
        out += [("ex", a, c, b) for b in range(2 * ATT[a]["kt"])]
        out.append(("pv_last", a, c))
        out.append(("ot", a, c))
    out += [("ao_t", a), ("oproj", a)]
    return out


SCHEDULE = (
    [("load",), ("ctx",), ("ln_first",), ("z_t", 0)]
    + attention_phases(0)
    + [("ln_res", 1), ("z_t", 1)]
    + attention_phases(1)
    + [("ln_res", 2), ("z_t", 2)]
    + [ph for half in range(2) for ph in [("ffn1", half, 0), ("ffn1", half, 1), ("ffn2", half)]]
    + [("ffn_out",), ("ln3",), ("ln_x",), ("z_fp8",), ("ffn8",)]
    + [("ln_x",), ("z_t", 0)]
    + attention_phases(2)
    + [("ln_x",), ("z_t", 0), ("router",), ("route",), ("w_t",), ("b_experts",)]
    + [("expert", tt, e) for tt in range(TT) for e in range(NE // 2)]
    + [("store",)]
)


def jobs_of(ph):
    name = ph[0]
    if name == "qs":
        return ["dve"] if ph[1] == 2 else ["act"]
    if name == "ex":
        return (["dve"] if ph[1] == 2 else ["act"]) * 2
    return {
        "ctx": ["dve"], "z_t": ["dve"], "vproj": ["act"], "qk": ["dve"], "ks": ["act"], "mx": ["dve"],
        "mt": ["act"], "ot": ["dve"], "ao_t": ["dve"], "oproj": ["dve"], "mq": ["dve"], "ffn1": ["act"], "z_fp8": ["dve"],
        "ffn8": ["act"], "router": ["dve"], "w_t": ["act"], "b_experts": ["dve"], "expert": ["dve"],
    }.get(name, [])


JOBS = []
FIRST_JOB = {}
for _i, _ph in enumerate(SCHEDULE):
    FIRST_JOB[_i] = len(JOBS)
    for _e in jobs_of(_ph):
        JOBS.append((_e, 1 + sum(1 for x in JOBS if x[0] == _e)))

TOTALS = {
    "loaded": 16 * 4,
    "stored": 16,
    "bank_full": len(JOBS),
    "dve_read": sum(1 for x in JOBS if x[0] == "dve"),
    "act_read": sum(1 for x in JOBS if x[0] == "act"),
    "dve_step": None,
    "act_step": None,
    "pool_step": None,
    "hi_ready": None,
    "feat_ready": None,
    "z_ready": None,
    "var_ready": None,
    "rstd_ready": None,
    "resid_ready": None,
    "negmax_ready": None,
    "pv_done": None,
    "o_full": None,
    "o_read": None,
    "ffn_read": None,
    "probs_ready": None,
    "gelu_hi": None,
    "gelu_lo": None,
    "fp8_ready": None,
    "fp16_ready": None,
    "logits_ready": None,
    "expl_ready": None,
    "weights_ready": None,
}
COUNTS = {
    "dve_step": 115, "act_step": 14, "pool_step": 2, "hi_ready": 15, "feat_ready": 2, "z_ready": 6,
    "var_ready": 7, "rstd_ready": 7, "resid_ready": 3, "negmax_ready": 6,
    "pv_done": 16, "o_full": 2, "o_read": 6, "ffn_read": 1, "probs_ready": 8, "gelu_hi": 2,
    "gelu_lo": 2, "fp8_ready": 1, "fp16_ready": 1, "logits_ready": 1, "expl_ready": 1,
    "weights_ready": 1,
}
TOTALS.update(COUNTS)


class Count:

    def __init__(self, eng, sems, it):
        self.eng, self.sems, self.it = eng, sems, it
        self.sent, self.taken, self.seen = {}, {}, {}

    def done(self, ins, name, s, by=1):
        ins.then_inc(self.sems[name][s], by)
        self.sent[name, s] = self.sent.get((name, s), 0) + by

    def at(self, name, s, k):
        if self.seen.get((name, s), 0) >= k:
            return
        self.seen[name, s] = k
        self.eng.wait_ge(self.sems[name][s], self.it * TOTALS[name] + k)

    def take(self, name, s, by=1):
        self.taken[name, s] = self.taken.get((name, s), 0) + by
        self.at(name, s, self.taken[name, s])

    def own(self, name, s):
        self.at(name, s, self.sent[name, s])

    def check(self, names):
        for name in names:
            for s in range(STREAMS):
                got = self.sent.get((name, s), 0)
                assert got == TOTALS[name], (name, s, got, TOTALS[name])


def build(nc, x, ctx_in, mask0, mask1, mask1_t, weights, w8_t, cols, rows, router_t, router_b, b_experts,
          identity, select, select_max, descending, out):
    ex = ExitStack()
    with ex:
        def sb(name, shape, dt=F32):
            return ex.enter_context(nc.sbuf_tensor(name, shape, dt))

        def both(name, shape, dt=F32):
            return [sb(f"{name}{s}", shape, dt) for s in range(STREAMS)]

        w_hi = sb("w_hi", [P, KC, NB, D], F32R)
        w_lo = sb("w_lo", [P, KC, NB, D], F32R)
        w8 = sb("w8", [P, KC, D], FP16)
        ident = sb("ident", [P, P])
        sel = sb("sel", [P, 4, NHP, P], F32R)
        sel_m = sb("sel_m", [2 * HC, NHP, P], F32R)
        col = sb("col", [P, NCOL + 1])
        row = sb("row", [P, NROW, D])
        wr_hi = sb("wr_hi", [P, KC, NE], F32R)
        wr_lo = sb("wr_lo", [P, KC, NE], F32R)
        rb = sb("rb", [P, NE])
        desc = sb("desc", [P, NE])
        bias_qk = sb("bias_qk", [P, TT, NK])
        low_rows = sb("low_rows", [P, S])
        some_q = sb("some_q", [P, S])
        some_p = sb("some_p", [P, TT])
        half_neg = sb("half_neg", [P, TT])
        X = both("X", [P, TT, D])
        R = both("R", [P, TT, D])
        Z = both("Z", [P, TT, D])
        feat_hi = both("feat_hi", [P, KC, S], F32R)
        feat_lo = both("feat_lo", [P, KC, S], F32R)
        ctx_hi = both("ctx_hi", [P, KC, NKP], F32R)
        ctx_lo = both("ctx_lo", [P, KC, NKP], F32R)
        q_hi = both("q_hi", [P, 2, S], F32R)
        q_lo = both("q_lo", [P, 2, S], F32R)
        Qs = both("Qs", [P, NHP, S], F32R)
        Ks = both("Ks", [P, NHP, S], F32R)
        Vx = both("Vx", [P, TT, H, HD + 1])
        probs = both("probs", [P, 4, 2 * S])
        att_t = both("att_t", [P, 2, S])
        mask_b = both("mask_b", [P, NK])
        mask_c = both("mask_c", [NK, 1])
        stats = both("stats", [P, TT, 6])
        mv = both("mv", [P, TT, 2])
        ve = both("ve", [P, TT])
        rstd = both("rstd", [P, TT])
        mxv = both("mxv", [P, TT, 2, NHP])
        negm = both("negm", [P, TT, 2, 2 * NHP], F32R)
        recip = both("recip", [P, TT, HC])

        bank = [[ex.enter_context(nc.psum_tensor(f"ring{s}{i}", [P, 512], F32)) for i in range(2)] for s in range(STREAMS)]
        obank = [[ex.enter_context(nc.psum_tensor(f"obank{s}{i}", [P, 512], F32)) for i in range(2)] for s in range(STREAMS)]

        sems = {n: [ex.enter_context(nc.semaphore(f"{n}{s}")) for s in range(STREAMS)] for n in TOTALS}
        setup_pool = ex.enter_context(nc.semaphore("setup_pool"))
        c_in = ex.enter_context(nc.semaphore("consts_loaded"))
        w_in = [ex.enter_context(nc.semaphore(f"raw_weights_loaded{i}")) for i in range(2)]
        w_hi_done = ex.enter_context(nc.semaphore("w_hi_done"))
        w_lo_done = ex.enter_context(nc.semaphore("w_lo_done"))
        setup_dve = ex.enter_context(nc.semaphore("setup_dve"))
        setup_act = ex.enter_context(nc.semaphore("setup_act"))
        count_done = ex.enter_context(nc.semaphore("unmasked_keys_counted"))

        bias_kq = low_rows[0:NK, :]
        b_ex = low_rows[96:96 + NE, :]
        max_t = [q_hi[s][0:2 * HC, 0, :] for s in range(STREAMS)]
        sc = [probs[s][:, 1, 0:8 * TT * NE].rearrange("p (n t e) -> p n t e", n=8, t=TT) for s in range(STREAMS)]
        sc1 = [probs[s][:, 1, 8 * TT * NE:8 * TT * NE + 8 * TT].rearrange("p (n t) -> p n t", n=8) for s in range(STREAMS)]
        wt = [probs[s][96:96 + NE, 2, 0:S] for s in range(STREAMS)]
        sm = [att_t[s][:, :, :].rearrange("p a b -> p (a b)")[:, 0:NHP * NK] for s in range(STREAMS)]
        m8_words = R[1][:, 0, 0:TT * MASK_WORDS].bitcast(I32).rearrange("p (t w) -> p t w", t=TT)
        m8 = R[1][:, 0, 0:TT * MASK_WORDS].bitcast(U8).rearrange("p (t k) -> p t k", t=TT)[:, :, 0:NK]
        m8t_words = R[1][0:NK, 1, 0:S // 4].bitcast(I32)
        m8t = R[1][0:NK, 1, 0:S // 4].bitcast(U8)
        sel_raw = [probs[i][:, 2:4, :].rearrange("p a b -> p (a b)") for i in range(2)]
        sel_m_raw = Z[0][0:2 * HC, :, :].rearrange("p a b -> p (a b)")
        router_raw = X[1][:, 0, 0:KC * NE].rearrange("p (k e) -> p k e", k=KC)
        feat = [probs[s][:, 0, :].rearrange("p (c t) -> p c t", c=KC) for s in range(STREAMS)]
        gelu = [probs[s][:, :, :].rearrange("p n (c t) -> p (n c) t", c=2) for s in range(STREAMS)]
        fp8f = [att_t[s][:, 0, 0:128].bitcast(FP8).rearrange("p (c t) -> p c t", c=KC) for s in range(STREAMS)]
        fp16f = [att_t[s][:, 1, :].bitcast(FP16).rearrange("p (c t) -> p c t", c=KC) for s in range(STREAMS)]
        out16 = [att_t[s][:, 0, :].bitcast(FP16).rearrange("p (t d) -> p t d", t=TT) for s in range(STREAMS)]
        raw = [probs[i][:, :, :].rearrange("p n m -> p (n m)")[:, 0:KC * WEIGHTS_STEP * D]
               .rearrange("p (k n) -> p k n", k=KC) for i in range(2)]
        NLOADS = NB // WEIGHTS_STEP
        N_CONST = 14

        def row3(j):
            return row[:, j, :].unsqueeze(1).to_broadcast([P, TT, D])

        block = ex.enter_context(nc.Block())

        @block.sync
        def _(eng):
            eng.dma_start(ident[:, :], identity).then_inc(c_in, 16)
            eng.dma_start(m8_words, mask1.rearrange("(t p) w -> p t w", p=P)).then_inc(c_in, 16)
            eng.dma_start(m8t_words, mask1_t).then_inc(c_in, 16)
            eng.dma_start(col[:, :], cols).then_inc(c_in, 16)
            eng.dma_start(rb[:, :], router_b).then_inc(c_in, 16)
            eng.dma_start(desc[:, :], descending).then_inc(c_in, 16)
            eng.dma_start(b_ex, b_experts).then_inc(c_in, 16)
            eng.dma_start(sel_raw[0], select[:, 0:4 * P * 2]).then_inc(c_in, 16)
            eng.dma_start(sel_raw[1], select[:, 4 * P * 2:4 * P * 4]).then_inc(c_in, 16)
            eng.dma_start(sel_m_raw, select_max).then_inc(c_in, 16)
            eng.dma_start(router_raw, router_t.rearrange("(k p) e -> p k e", p=P)).then_inc(c_in, 16)
            eng.dma_start(att_t[0][:, :, :], w8_t.rearrange("(k p) f -> p k f", p=P)).then_inc(c_in, 16)
            eng.dma_start(row[:, :, :], rows[:, 0:NROW, :]).then_inc(c_in, 16)
            eng.dma_start(X[0][:, :, :], rows[:, NROW:NROW + 2, :]).then_inc(c_in, 16)
            for n in range(NLOADS):
                if n >= 2:
                    eng.wait_ge(w_lo_done, n - 1)
                eng.dma_start(raw[n % 2], weights[:, n * WEIGHTS_STEP * D:(n + 1) * WEIGHTS_STEP * D]
                              .rearrange("(k p) n -> p k n", p=P)).then_inc(w_in[n % 2], 16)
            eng.wait_ge(setup_act, 4)
            eng.wait_ge(setup_pool, 9)
            eng.wait_ge(setup_dve, 5)
            with eng.Fori(0, ITERS) as it:
                c = Count(eng, sems, it)
                for ph in SCHEDULE:
                    for s in range(STREAMS):
                        if ph[0] == "load":
                            c.at("stored", s, 16)
                            c.done(eng.dma_start(X[s][:, :, :], x[it * STREAMS + s].rearrange("(t p) d -> p t d", p=P)), "loaded", s, 16)
                            c.done(eng.dma_start(att_t[s][0:NK, 0, :], ctx_in[it * STREAMS + s]), "loaded", s, 16)
                            c.done(eng.dma_start(mask_b[s][:, :], mask0[it * STREAMS + s].partition_broadcast(P)), "loaded", s, 16)
                            c.done(eng.dma_start(mask_c[s][:, :], mask0[it * STREAMS + s].rearrange("(k a) -> k a", a=1)), "loaded", s, 16)
                        elif ph[0] == "store":
                            c.at("dve_read", s, TOTALS["dve_read"])
                            c.done(eng.dma_start(out[it * STREAMS + s].rearrange("(t p) d -> p t d", p=P), X[s][:, :, :]), "stored", s, 16)
                c.check(["loaded", "stored"])
            for s in range(STREAMS):
                eng.wait_ge(sems["stored"][s], 16 * (ITERS + 1))

        @block.gpsimd
        def _(eng):
            g = nc.gpsimd
            g.memset(half_neg[:, :], -0.5).then_inc(setup_pool, 1)
            for s in range(STREAMS):
                g.memset(ve[s][:, :], 0.0).then_inc(sems["stored"][s], 16)
            for s in range(STREAMS):
                g.memset(Vx[s][:, :, :, :], 1.0).then_inc(setup_pool, 1)
                g.memset(ctx_hi[s][:, :, :].bitcast(F32), 0.0).then_inc(setup_pool, 1)
                g.memset(ctx_lo[s][:, :, :].bitcast(F32), 0.0).then_inc(setup_pool, 1)
            eng.wait_ge(c_in, 16 * N_CONST)
            g.tensor_tensor(row[:, R_E1, :], row[:, R_E1, :], X[0][:, 0, :], ALU.add).then_inc(setup_pool, 1)
            g.tensor_tensor(row[:, R_E2, :], row[:, R_E2, :], X[0][:, 1, :], ALU.add).then_inc(setup_pool, 1)
            eng.wait_ge(setup_pool, 9)
            with eng.Fori(0, ITERS) as it:
                c = Count(eng, sems, it)

                def inverse_root(s):
                    c.take("var_ready", s)
                    c.done(g.tensor_tensor(rstd[s][:, :], ve[s][:, :], half_neg[:, :], ALU.pow), "rstd_ready", s)

                for ph in SCHEDULE:
                    for s in range(STREAMS):
                        if ph[0] in ("ln_first", "ln_res", "ln3", "ln_x"):
                            inverse_root(s)
                        if ph[0] == "ln_first":
                            c.take("z_ready", s)
                            c.done(g.tensor_tensor(R[s][:, :, :], Z[s][:, :, :], row3(R_COB), ALU.add), "resid_ready", s)
                        elif ph[0] == "ln_res":
                            c.take("z_ready", s)
                            c.done(g.tensor_tensor(R[s][:, :, :], Z[s][:, :, :], row3(R_G1 if ph[1] == 1 else R_G2), ALU.mult), "pool_step", s)
                            c.own("pool_step", s)
                            c.done(g.tensor_tensor(R[s][:, :, :], R[s][:, :, :], row3(R_E1 if ph[1] == 1 else R_E2), ALU.add), "resid_ready", s)
                for s in range(STREAMS):
                    c.at("stored", s, 2 * 16)
                c.check(["pool_step", "rstd_ready", "resid_ready"])

        @block.scalar
        def _(eng):
            a_ = nc.scalar
            eng.wait_ge(c_in, 16 * N_CONST)
            a_.activation(sel[:, 0:2, :, :].rearrange("p w h d -> p (w h d)"), sel_raw[0], ACT.Copy).then_inc(setup_act, 1)
            a_.activation(sel[:, 2:4, :, :].rearrange("p w h d -> p (w h d)"), sel_raw[1], ACT.Copy).then_inc(setup_act, 1)
            a_.activation(sel_m[:, :, :].rearrange("p h k -> p (h k)"), sel_m_raw, ACT.Copy).then_inc(setup_act, 1)
            a_.activation(wr_hi[:, :, :], router_raw, ACT.Copy).then_inc(setup_act, 1)
            for n in range(NLOADS):
                eng.wait_ge(w_in[n % 2], 16 * (n // 2 + 1))
                a_.activation(w_hi[:, :, n * WEIGHTS_STEP:(n + 1) * WEIGHTS_STEP, :],
                              raw[n % 2].rearrange("p k (b d) -> p k b d", d=D), ACT.Copy).then_inc(w_hi_done, 1)
            eng.wait_ge(setup_pool, 9)
            eng.wait_ge(setup_dve, 5)
            eng.wait_ge(w_lo_done, NLOADS)
            with eng.Fori(0, ITERS) as it:
                c = Count(eng, sems, it)
                act_jobs = [0] * STREAMS
                blocks = [0] * STREAMS
                for i, ph in enumerate(SCHEDULE):
                    name = ph[0]
                    for s in range(STREAMS):
                        n = FIRST_JOB[i]

                        def full(k=0):
                            c.at("bank_full", s, n + k + 1)
                            return bank[s][(n + k) % 2]

                        if name == "ctx":
                            b = full()
                            c.done(a_.activation(ctx_hi[s][:, :, 0:NK], b[:, 0:2 * NK].rearrange("p (c k) -> p c k", c=KC), ACT.Copy), "hi_ready", s)
                        elif name == "z_t":
                            if ph[1]:
                                c.take("feat_ready", s)
                                c.done(a_.activation(feat_hi[s][:, :, :], feat[s], ACT.Copy), "hi_ready", s)
                            else:
                                b = full()
                                c.done(a_.activation(feat_hi[s][:, :, :], b[:, :].rearrange("p (c t) -> p c t", c=KC), ACT.Copy), "hi_ready", s)
                        elif name == "vproj":
                            b = full()
                            kt = ATT[ph[1]]["kt"]
                            np_ = P if kt == 2 else NK
                            c.done(a_.activation(Vx[s][0:np_, 0:kt, :, 0:HD],
                                                 b[0:np_, 0:kt * D].rearrange("p (t h d) -> p t h d", t=kt, d=HD), ACT.Copy), "act_read", s)
                        elif name == "qk":
                            b = full()
                            at, ch = ATT[ph[1]], ph[2]
                            nk = NKP if at["ctx"] else S
                            c.done(a_.activation(q_hi[s][:, 0, :], b[:, 0:S], ACT.Identity, bias=col[:, at["bq"] + ch:at["bq"] + ch + 1]), "act_step", s)
                            c.done(a_.activation(q_hi[s][:, 1, 0:nk], b[:, S:S + nk], ACT.Identity, bias=col[:, at["bk"] + ch:at["bk"] + ch + 1]), "hi_ready", s)
                        elif name == "ks":
                            b = full()
                            if ATT[ph[1]]["ctx"]:
                                o, v = Ks[s][:, :, 0:NKP], b[:, 0:NHP * NKP].rearrange("p (h k) -> p h k", h=NHP)
                            else:
                                o, v = Ks[s][:, 2 * ph[3]:2 * ph[3] + 2, :], b[:, :].rearrange("p (h k) -> p h k", h=2)
                            c.done(a_.activation(o, v, ACT.Identity, bias=col[:, NCOL:NCOL + 1]), "act_read", s)
                        elif name == "qs" and ph[1] != 2:
                            b = full()
                            c.done(a_.activation(Qs[s][:, 2 * ph[3]:2 * ph[3] + 2, :], b[:, :].rearrange("p (h k) -> p h k", h=2), ACT.Copy), "act_read", s)
                        elif name == "mt":
                            b = full()
                            c.done(a_.activation(max_t[s], b[0:2 * HC, 0:S], ACT.Copy), "act_read", s)
                        elif name == "ex":
                            at = ATT[ph[1]]
                            np_ = P if at["kt"] == 2 else NK
                            for k in range(2):
                                slot = 2 * (blocks[s] % 2) + k
                                if ph[1] == 2:
                                    c.at("dve_read", s, JOBS[n + k][1])
                                    src = probs[s][0:np_, slot, :]
                                else:
                                    src = full(k)[0:np_, :]
                                    if blocks[s] >= 2 and k == 0:
                                        c.at("pv_done", s, blocks[s] - 1)
                                if ph[1] == 0:
                                    ins = a_.activation(probs[s][0:np_, slot, :], src, ACT.Exp, scale=QSCALE, bias=mask_c[s][:, :])
                                else:
                                    ins = a_.activation(probs[s][0:np_, slot, :], src, ACT.Exp, scale=QSCALE)
                                c.done(ins, "probs_ready" if ph[1] == 2 else "act_read", s)
                            blocks[s] += 1
                        elif name == "ot":
                            c.at("pv_done", s, blocks[s])
                            c.done(a_.activation(att_t[s][:, :, :], obank[s][ph[2]][:, :].rearrange("p (c t) -> p c t", c=2), ACT.Copy), "o_read", s)
                        elif name == "ao_t":
                            b = full()
                            bv = ATT[ph[1]]["bv"]
                            c.done(a_.activation(feat_hi[s][:, 0, :], b[:, 0:S], ACT.Identity, bias=col[:, bv:bv + 1]), "act_step", s)
                            c.done(a_.activation(feat_hi[s][:, 1, :], b[:, S:2 * S], ACT.Identity, bias=col[:, bv + 1:bv + 2]), "hi_ready", s)
                        elif name == "ffn1":
                            b = full()
                            f = 4 * ph[1] + 2 * ph[2]
                            c.done(a_.activation(gelu[s][:, f, :], b[:, 0:S], ACT.Gelu, bias=col[:, B_FI + f:B_FI + f + 1]), "act_step", s)
                            c.done(a_.activation(gelu[s][:, f + 1, :], b[:, S:2 * S], ACT.Gelu, bias=col[:, B_FI + f + 1:B_FI + f + 2]), "act_read", s)
                            if ph[2] == 1:
                                c.own("act_read", s)
                                if ph[1]:
                                    c.at("o_full", s, 1)
                                c.done(a_.activation(Qs[s][:, :, :], gelu[s][:, 4 * ph[1]:4 * ph[1] + 4, :], ACT.Copy), "gelu_hi", s)
                        elif name == "z_fp8":
                            c.take("fp8_ready", s)
                            c.done(a_.activation(att_t[s][:, 0, S - 1:S], col[:, 0:1], ACT.Copy), "act_step", s)
                            c.done(a_.activation(fp16f[s], fp8f[s], ACT.Copy), "fp16_ready", s)
                        elif name == "ffn8":
                            b = full()
                            c.own("act_step", s)
                            c.done(a_.activation(out16[s], b[:, :].rearrange("p (t d) -> p t d", t=TT), ACT.Copy), "act_read", s)
                        elif name == "route":
                            c.take("logits_ready", s)
                            c.done(a_.activation(sc[s][:, 1, :, :], sc[s][:, 0, :, :], ACT.Exp), "expl_ready", s)
                        elif name == "w_t":
                            b = full()
                            c.done(a_.activation(wt[s], b[0:NE, 0:S], ACT.Copy), "act_read", s)
                for s in range(STREAMS):
                    c.at("stored", s, 2 * 16)
                c.check(["act_step", "act_read", "hi_ready", "o_read", "probs_ready", "fp16_ready", "expl_ready"])

        @block.vector
        def _(eng):
            v = nc.vector
            n_set = [0]

            def setup(ins):
                n_set[0] += 1
                ins.then_inc(setup_dve, 1)
                eng.wait_ge(setup_dve, n_set[0])

            for s in range(STREAMS):
                for i in range(2):
                    setup(v.memset(obank[s][i][:, :], 0.0))
            eng.wait_ge(c_in, 16 * N_CONST)
            eng.wait_ge(setup_act, 4)
            eng.wait_ge(setup_pool, 9)
            setup(v.tensor_tensor(wr_lo[:, :, :], router_raw, wr_hi[:, :, :].bitcast(F32), ALU.subtract))
            mag = Z[0][:, :, :]
            small = att_t[1][:, :, :]
            large = Z[1][:, :, :]
            f8 = R[0][:, 1, 0:128].bitcast(FP8).rearrange("p (k f) -> p k f", k=KC)
            raw8 = att_t[0][:, :, :]
            setup(v.tensor_scalar(mag, raw8, 16.0, -16.0, ALU.min, ALU.max))
            setup(v.tensor_copy(f8, mag, saturate=False))
            setup(v.tensor_copy(small, f8))
            setup(v.tensor_scalar(mag, raw8, FP8_MAX, -FP8_MAX, ALU.min, ALU.max))
            setup(v.tensor_scalar(large, mag, 0.5, None, ALU.mult))
            setup(v.tensor_copy(f8, large, saturate=False))
            setup(v.tensor_copy(large, f8))
            setup(v.tensor_scalar(large, large, 2.0, None, ALU.mult))
            setup(v.tensor_tensor(large, large, small, ALU.subtract))
            setup(v.tensor_tensor(mag, mag, mag, ALU.mult))
            setup(v.tensor_scalar(mag, mag, 256.0, None, ALU.is_gt))
            setup(v.tensor_tensor(large, large, mag, ALU.mult))
            setup(v.tensor_tensor(w8[:, :, :], small, large, ALU.add))
            mf = R[0][:, 1, 0:TT * NK].rearrange("p (t k) -> p t k", t=TT)
            mft = R[0][0:NK, 0, :]
            setup(v.tensor_copy(mf, m8))
            setup(v.tensor_copy(mft, m8t))
            setup(v.tensor_reduce(some_p[:, :], mf, AX.X, ALU.max))
            setup(v.tensor_scalar(mf, mf, -NEG, NEG, ALU.mult, ALU.add))
            for t in range(TT):
                setup(v.tensor_scalar(bias_qk[:, t, :], mf[:, t, :], some_p[:, t:t + 1], None, ALU.mult))
            eng.wait_ge(count_done, 1)
            setup(v.tensor_scalar(some_q[:, :], bank[0][0][:, 0:S], 1.0, None, ALU.min))
            setup(v.tensor_scalar(mft, mft, -NEG, NEG, ALU.mult, ALU.add))
            setup(v.tensor_tensor(bias_kq, mft, some_q[0:NK, :], ALU.mult))
            for n in range(NLOADS):
                eng.wait_ge(w_hi_done, n + 1)
                v.tensor_tensor(w_lo[:, :, n * WEIGHTS_STEP:(n + 1) * WEIGHTS_STEP, :],
                                raw[n % 2].rearrange("p k (b d) -> p k b d", d=D),
                                w_hi[:, :, n * WEIGHTS_STEP:(n + 1) * WEIGHTS_STEP, :].bitcast(F32),
                                ALU.subtract).then_inc(w_lo_done, 1)
            with eng.Fori(0, ITERS) as it:
                c = Count(eng, sems, it)

                def step(s, ins):
                    c.done(ins, "dve_step", s)

                def link(s, ins):
                    c.done(ins, "dve_step", s)
                    c.own("dve_step", s)

                def normalise(s, src, signal="z_ready"):
                    for t in range(TT):
                        step(s, v.bn_stats(stats[s][:, t, :], src[:, t, :]))
                    c.own("dve_step", s)
                    step(s, v.memset(recip[s][:, 0, 0:1], 0.0))
                    for t in range(TT):
                        step(s, v.bn_aggr(mv[s][:, t, :], stats[s][:, t, :]))
                    c.own("dve_step", s)
                    c.done(v.tensor_scalar(ve[s][:, :], mv[s][:, :, 1], EPS, None, ALU.add), "var_ready", s)
                    c.take("rstd_ready", s)
                    for t in range(TT):
                        ins = v.tensor_scalar(Z[s][:, t, :], src[:, t, :], mv[s][:, t, 0:1], rstd[s][:, t:t + 1], ALU.subtract, ALU.mult)
                        if t < TT - 1:
                            step(s, ins)
                        else:
                            c.done(ins, signal, s)

                def low_part(s, o, src, hi, bias=None):
                    if bias is None:
                        return v.tensor_tensor(o, src, hi.bitcast(F32), ALU.subtract)
                    return v.scalar_tensor_tensor(o, src, bias, hi.bitcast(F32), ALU.add, ALU.subtract)

                for i, ph in enumerate(SCHEDULE):
                    name = ph[0]
                    n = FIRST_JOB[i]
                    for s in range(STREAMS):
                        def full(k=0):
                            c.at("bank_full", s, n + k + 1)
                            return bank[s][(n + k) % 2]

                        if name == "load":
                            c.take("loaded", s, 64)
                            link(s, v.tensor_scalar(mask_b[s][:, :], mask_b[s][:, :], 1.0 / QSCALE, NEG, ALU.mult, ALU.max))
                        elif name == "ctx":
                            b = full()
                            c.take("hi_ready", s)
                            c.done(low_part(s, ctx_lo[s][:, :, 0:NK], b[:, 0:2 * NK].rearrange("p (c k) -> p c k", c=KC), ctx_hi[s][:, :, 0:NK]), "dve_read", s)
                        elif name in ("ln_first", "ln_x"):
                            normalise(s, X[s])
                        elif name == "ln_res":
                            normalise(s, Z[s])
                        elif name == "z_t":
                            b = full()
                            bv = b[:, :].rearrange("p (c t) -> p c t", c=KC)
                            if ph[1]:
                                g_, e_ = (G_CO, E_CO) if ph[1] == 1 else (G_SO, E_SO)
                                for ch in range(KC):
                                    ins = v.tensor_scalar(feat[s][:, ch, :], bv[:, ch, :], col[:, g_ + ch:g_ + ch + 1], col[:, e_ + ch:e_ + ch + 1], ALU.mult, ALU.add)
                                    if ch < KC - 1:
                                        step(s, ins)
                                    else:
                                        c.done(ins, "feat_ready", s)
                                c.own("feat_ready", s)
                                bv = feat[s]
                            c.take("hi_ready", s)
                            c.done(low_part(s, feat_lo[s][:, :, :], bv, feat_hi[s][:, :, :]), "dve_read", s)
                        elif name == "qk":
                            b = full()
                            at, ch = ATT[ph[1]], ph[2]
                            nk = NKP if at["ctx"] else S
                            c.take("hi_ready", s)
                            step(s, low_part(s, q_lo[s][:, 0, :], b[:, 0:S], q_hi[s][:, 0, :], col[:, at["bq"] + ch:at["bq"] + ch + 1]))
                            c.done(low_part(s, q_lo[s][:, 1, 0:nk], b[:, S:S + nk], q_hi[s][:, 1, 0:nk], col[:, at["bk"] + ch:at["bk"] + ch + 1]), "dve_read", s)
                        elif name == "qs" and ph[1] == 2:
                            b = full()
                            c.done(v.tensor_tensor(Qs[s][:, 2 * ph[3]:2 * ph[3] + 2, :], b[:, :].rearrange("p (h k) -> p h k", h=2),
                                                   some_q[:, :].unsqueeze(1).to_broadcast([P, 2, S]), ALU.mult), "dve_read", s)
                        elif name == "mx":
                            b = full()
                            if ATT[ph[1]]["ctx"]:
                                p, q = ph[3] // TT, ph[3] % TT
                                bias = mask_b[s][:, :] if ph[1] == 0 else bias_qk[:, q, :]
                                smv = sm[s].rearrange("p (h k) -> p h k", h=NHP)
                                if ph[3]:
                                    c.own("dve_step", s)
                                c.done(v.tensor_tensor(smv, b[:, 0:NHP * NKP].rearrange("p (h k) -> p h k", h=NHP)[:, :, 0:NK],
                                                       bias.unsqueeze(1).to_broadcast([P, NHP, NK]), ALU.add), "dve_read", s)
                                c.own("dve_read", s)
                                step(s, v.tensor_reduce(mxv[s][:, q, p, :], smv, AX.X, ALU.max))
                            else:
                                h = ph[3]
                                c.done(v.tensor_reduce(mxv[s][:, :, h % 2, h // 2], b[:, :].rearrange("p (t k) -> p t k", t=TT), AX.X, ALU.max), "dve_read", s)
                        elif name == "mt":
                            c.own("dve_step" if ATT[ph[1]]["ctx"] else "dve_read", s)
                            mm = mxv[s][:, :, :, :].rearrange("p t a h -> p t (a h)")
                            link(s, v.tensor_scalar(negm[s][:, :, 0, :], mm, -1.0, None, ALU.mult))
                            c.done(v.scalar_tensor_tensor(negm[s][:, :, 1, :], mm, -1.0, negm[s][:, :, 0, :].bitcast(F32), ALU.mult, ALU.subtract), "negmax_ready", s)
                        elif name == "mq":
                            b = full()
                            qv = Qs[s][:, 2 * ph[3]:2 * ph[3] + 2, :]
                            c.done(v.tensor_tensor(qv, qv.bitcast(F32), b[:, :].rearrange("p (h k) -> p h k", h=2), ALU.add), "dve_read", s)
                        elif name == "ex" and ph[1] == 2:
                            blk = 12 + 2 * ph[2] + ph[3]
                            for k in range(2):
                                b = full(k)
                                if k == 0:
                                    c.at("pv_done", s, blk - 1)
                                c.done(v.tensor_tensor(probs[s][0:NK, 2 * (blk % 2) + k, :].rearrange("p (h q) -> p h q", h=2),
                                                       b[0:NK, :].rearrange("p (h q) -> p h q", h=2),
                                                       bias_kq.unsqueeze(1).to_broadcast([NK, 2, S]), ALU.add), "dve_read", s)
                        elif name == "ot":
                            b = full()
                            bt = b[:, :].rearrange("p (t g w) -> p t g w", t=TT, w=2 * HD)
                            if ph[2] == 0 and ph[1] < 2:
                                c.take("resid_ready", s)
                            link(s, v.reciprocal(recip[s][:, :, :], bt[:, :, :, HD]))
                            c.done(v.tensor_tensor(Z[s][:, :, ph[2] * P:(ph[2] + 1) * P].rearrange("p t (g d) -> p t g d", d=HD),
                                                   bt[:, :, :, 0:HD], recip[s][:, :, :].unsqueeze(3).to_broadcast([P, TT, HC, HD]), ALU.mult), "dve_read", s)
                        elif name == "ao_t":
                            b = full()
                            bv = ATT[ph[1]]["bv"]
                            c.take("hi_ready", s)
                            step(s, low_part(s, feat_lo[s][:, 0, :], b[:, 0:S], feat_hi[s][:, 0, :], col[:, bv:bv + 1]))
                            c.done(low_part(s, feat_lo[s][:, 1, :], b[:, S:2 * S], feat_hi[s][:, 1, :], col[:, bv + 1:bv + 2]), "dve_read", s)
                        elif name == "oproj":
                            b = full()
                            bv = b[:, :].rearrange("p (t d) -> p t d", t=TT)
                            if ph[1] < 2:
                                c.done(v.tensor_tensor(Z[s][:, :, :], bv, R[s][:, :, :], ALU.add), "dve_read", s)
                                c.own("dve_read", s)
                            else:
                                c.done(v.tensor_tensor(Z[s][:, :, :], bv, row3(R_LOB), ALU.add), "dve_read", s)
                                c.own("dve_read", s)
                                link(s, v.tensor_tensor(X[s][:, :, :], X[s][:, :, :], Z[s][:, :, :], ALU.add))
                        elif name == "ffn1" and ph[2] == 1:
                            c.take("gelu_hi", s)
                            h = ph[1]
                            c.done(low_part(s, Ks[s][:, :, :], gelu[s][:, 4 * h:4 * h + 4, :], Qs[s][:, :, :]), "gelu_lo", s)
                        elif name == "ffn_out":
                            c.take("resid_ready", s)
                            c.at("o_full", s, 2)
                            step(s, v.tensor_tensor(Z[s][:, 0, :], obank[s][0][:, 0:D], R[s][:, 0, :], ALU.add))
                            c.done(v.tensor_tensor(Z[s][:, 1, :], obank[s][1][:, 0:D], R[s][:, 1, :], ALU.add), "ffn_read", s)
                            c.own("ffn_read", s)
                        elif name == "ln3":
                            normalise(s, Z[s], "dve_step")
                            c.own("dve_step", s)
                            link(s, v.tensor_tensor(Z[s][:, :, :], Z[s][:, :, :], row3(R_G3), ALU.mult))
                            link(s, v.tensor_tensor(Z[s][:, :, :], Z[s][:, :, :], row3(R_E3), ALU.add))
                            link(s, v.tensor_tensor(X[s][:, :, :], X[s][:, :, :], Z[s][:, :, :], ALU.add))
                        elif name == "z_fp8":
                            b = full()
                            c.done(v.tensor_scalar(feat[s], b[:, :].rearrange("p (c t) -> p c t", c=KC), FP8_MAX, -FP8_MAX, ALU.min, ALU.max), "dve_read", s)
                            c.own("dve_read", s)
                            step(s, v.memset(recip[s][:, 0, 0:1], 0.0))
                            c.done(v.tensor_copy(fp8f[s], feat[s], saturate=False), "fp8_ready", s)
                        elif name == "ffn8":
                            c.at("act_read", s, JOBS[n][1])
                            link(s, v.tensor_tensor(Z[s][:, :, :], out16[s], row3(R_FFB), ALU.add))
                            link(s, v.tensor_tensor(X[s][:, :, :], X[s][:, :, :], Z[s][:, :, :], ALU.add))
                        elif name == "router":
                            b = full()
                            L = sc[s][:, 0, :, :]
                            c.done(v.tensor_tensor(L, b[:, 0:TT * NE].rearrange("p (t e) -> p t e", t=TT), rb[:, :].unsqueeze(1).to_broadcast([P, TT, NE]), ALU.add), "dve_read", s)
                            c.own("dve_read", s)
                            link(s, v.tensor_reduce(sc1[s][:, 0, :], L, AX.X, ALU.max))
                            c.done(v.tensor_tensor(L, L, sc1[s][:, 0, :].unsqueeze(2).to_broadcast([P, TT, NE]), ALU.subtract), "logits_ready", s)
                        elif name == "route":
                            def wide(j):
                                return sc1[s][:, j, :].unsqueeze(2).to_broadcast([P, TT, NE])
                            t8 = [sc[s][:, j, :, :] for j in range(8)]
                            E = t8[1]
                            dsc = desc[:, :].unsqueeze(1).to_broadcast([P, TT, NE])
                            c.take("expl_ready", s)
                            step(s, v.tensor_reduce(sc1[s][:, 1, :], E, AX.X, ALU.add))
                            link(s, v.tensor_reduce(sc1[s][:, 2, :], E, AX.X, ALU.max))
                            step(s, v.reciprocal(sc1[s][:, 6, :], sc1[s][:, 1, :]))
                            link(s, v.tensor_tensor(t8[2], E, wide(2), ALU.is_equal))
                            link(s, v.tensor_tensor(t8[2], t8[2], dsc, ALU.mult))
                            link(s, v.tensor_reduce(sc1[s][:, 3, :], t8[2], AX.X, ALU.max))
                            link(s, v.tensor_tensor(t8[3], t8[2], wide(3), ALU.is_equal))
                            link(s, v.scalar_tensor_tensor(t8[4], t8[3], -2.0, E, ALU.mult, ALU.add))
                            link(s, v.tensor_reduce(sc1[s][:, 4, :], t8[4], AX.X, ALU.max))
                            link(s, v.tensor_tensor(t8[5], t8[4], wide(4), ALU.is_equal))
                            link(s, v.tensor_tensor(t8[5], t8[5], dsc, ALU.mult))
                            link(s, v.tensor_reduce(sc1[s][:, 5, :], t8[5], AX.X, ALU.max))
                            link(s, v.tensor_tensor(t8[6], t8[5], wide(5), ALU.is_equal))
                            link(s, v.tensor_tensor(t8[6], t8[6], t8[3], ALU.add))
                            link(s, v.tensor_tensor(t8[6], t8[6], E, ALU.mult))
                            c.done(v.tensor_tensor(t8[7], t8[6], wide(6), ALU.mult), "weights_ready", s)
                            c.own("weights_ready", s)
                        elif name == "b_experts":
                            b = full()
                            c.done(v.tensor_tensor(X[s][:, :, :], X[s][:, :, :], b[:, :].rearrange("p (t d) -> p t d", t=TT), ALU.add), "dve_read", s)
                            c.own("dve_read", s)
                        elif name == "expert":
                            b = full()
                            t, e = ph[1], 2 * ph[2]
                            link(s, v.scalar_tensor_tensor(X[s][:, t, :], b[:, 0:D], sc[s][:, 7, t, e:e + 1], X[s][:, t, :], ALU.mult, ALU.add))
                            c.done(v.scalar_tensor_tensor(X[s][:, t, :], b[:, D:2 * D], sc[s][:, 7, t, e + 1:e + 2], X[s][:, t, :], ALU.mult, ALU.add), "dve_read", s)
                            c.own("dve_read", s)
                for s in range(STREAMS):
                    c.at("stored", s, 2 * 16)
                c.check(["dve_read", "dve_step", "z_ready", "var_ready", "feat_ready", "negmax_ready", "gelu_lo",
                         "ffn_read", "fp8_ready", "logits_ready", "weights_ready"])

        @block.tensor
        def _(eng):
            mm, tr = nc.tensor.matmul, nc.tensor.transpose
            eng.wait_ge(setup_dve, 20)
            eng.wait_ge(setup_pool, 9)
            all_ones = Vx[0][0:NK, 0, 0:8, :].rearrange("p h d -> p (h d)")[:, 0:P]
            mm(bank[0][0][:, 0:S], all_ones[:, :], R[0][0:NK, 0, :], start=True, stop=True).then_inc(count_done, 1)
            eng.wait_ge(w_lo_done, NLOADS)
            eng.wait_ge(setup_act, 4)
            with eng.Fori(0, ITERS) as it:
                c = Count(eng, sems, it)
                blocks = [0] * STREAMS

                def product(o, left, right, ws, acc=False, end=True):
                    (lh, ll), (rh, rl) = left, right
                    n = len(ws)
                    last = None
                    for j, k in enumerate(ws):
                        for m, (l, r) in enumerate(((ll, rh), (lh, rl), (lh, rh))):
                            last = mm(o, l(k), r(k), start=(not acc and j == 0 and m == 0), stop=(end and j == n - 1 and m == 2))
                    return last

                def W(which, w, a, b):
                    return tuple((lambda k, t=t: t[:, k, w, a:b]) for t in which)

                WW = (w_hi, w_lo)

                for i, ph in enumerate(SCHEDULE):
                    name = ph[0]
                    for s in range(STREAMS):
                        n = FIRST_JOB[i]
                        FF = (feat_hi[s], feat_lo[s])
                        CC = (ctx_hi[s], ctx_lo[s])

                        def feat_cols(a, b, t=FF):
                            return tuple((lambda k, u=u: u[:, k, a:b]) for u in t)

                        def free(k=0):
                            j = n + k
                            if j >= 2:
                                e, cnt = JOBS[j - 2]
                                c.at(f"{e}_read", s, cnt)
                            return bank[s][j % 2]

                        def produced(ins):
                            c.done(ins, "bank_full", s)

                        def last_read():
                            e, cnt = JOBS[n - 1]
                            c.at(f"{e}_read", s, cnt)

                        def pv(a, ch, blk, gb):
                            at = ATT[a]
                            kt, j = blk % at["kt"], blk // at["kt"]
                            np_ = P if at["kt"] == 2 else NK
                            for g in range(4):
                                head = ch * HC + 4 * j + g
                                src = probs[s][0:np_, 2 * (gb % 2) + g % 2, (g // 2) * S:(g // 2 + 1) * S]
                                last = mm(obank[s][ch][32 * g:32 * g + HD + 1, j * S:(j + 1) * S], Vx[s][0:np_, kt, head, :], src,
                                          start=(kt == 0), stop=(kt == at["kt"] - 1), tile_position=(0, 32 * g), skip_group_check=True)
                            c.done(last, "pv_done", s)

                        if name == "ctx":
                            c.take("loaded", s, 64)
                            b = free()
                            for k in range(KC):
                                last = tr(b[:, k * NK:(k + 1) * NK], att_t[s][0:NK, 0, k * P:(k + 1) * P], ident[0:NK, 0:NK])
                            produced(last)
                        elif name in ("z_t", "z_fp8", "ao_t"):
                            if name == "ao_t":
                                last_read()
                            else:
                                c.take("z_ready", s)
                            b = free()
                            for k in range(KC):
                                for t in range(TT):
                                    last = tr(b[:, k * S + t * P:k * S + (t + 1) * P], Z[s][:, t, k * P:(k + 1) * P], ident[:, :])
                            produced(last)
                        elif name == "vproj":
                            at = ATT[ph[1]]
                            last_read()
                            b = free()
                            for t in range(at["kt"]):
                                if at["ctx"]:
                                    last = product(b[0:NK, 0:D], feat_cols(0, NK, CC), W(WW, at["v"], 0, D), range(KC))
                                else:
                                    last = product(b[:, t * D:(t + 1) * D], feat_cols(t * P, (t + 1) * P), W(WW, at["v"], 0, D), range(KC))
                            produced(last)
                        elif name == "qk":
                            at, ch = ATT[ph[1]], ph[2]
                            b = free()
                            product(b[:, 0:S], W(WW, at["q"], ch * P, (ch + 1) * P), feat_cols(0, S), range(KC))
                            if at["ctx"]:
                                last = product(b[:, S:S + NKP], W(WW, at["k"], ch * P, (ch + 1) * P), feat_cols(0, NKP, CC), range(KC))
                            else:
                                last = product(b[:, S:2 * S], W(WW, at["k"], ch * P, (ch + 1) * P), feat_cols(0, S), range(KC))
                            produced(last)
                        elif name in ("ks", "qs"):
                            key = name == "ks"
                            if key and ph[3] == 0:
                                last_read()
                            b = free()
                            wide = NKP if key and ATT[ph[1]]["ctx"] else S
                            hps = range(NHP) if wide == NKP else (2 * ph[3], 2 * ph[3] + 1)
                            for j, hp in enumerate(hps):
                                o = b[:, j * wide:(j + 1) * wide]
                                mm(o, sel[:, 2 * key, hp, :], q_hi[s][:, int(key), 0:wide], start=True, stop=False)
                                last = mm(o, sel[:, 2 * key + 1, hp, :], q_lo[s][:, int(key), 0:wide], start=False, stop=True)
                            produced(last)
                        elif name == "mx":
                            if ph[3] == 0:
                                last_read()
                                c.at(JOBS[n - 2][0] + "_read", s, JOBS[n - 2][1])
                            b = free()
                            if ATT[ph[1]]["ctx"]:
                                p, q = ph[3] // TT, ph[3] % TT
                                if ph[3] == 0:
                                    c.at(JOBS[n - 3][0] + "_read", s, JOBS[n - 3][1])
                                for hp in range(NHP):
                                    last = mm(b[:, hp * NKP:(hp + 1) * NKP], Qs[s][64 * p:64 * p + 64, hp, q * P:(q + 1) * P],
                                              Ks[s][64 * p:64 * p + 64, hp, 0:NKP], start=True, stop=True)
                            else:
                                p, hp = ph[3] % 2, ph[3] // 2
                                for q in range(TT):
                                    last = mm(b[:, q * S:(q + 1) * S], Qs[s][64 * p:64 * p + 64, hp, q * P:(q + 1) * P],
                                              Ks[s][64 * p:64 * p + 64, hp, :], start=True, stop=True)
                            produced(last)
                        elif name == "mt":
                            c.take("negmax_ready", s)
                            b = free()
                            for t in range(TT):
                                last = tr(b[0:2 * HC, t * P:(t + 1) * P], negm[s][:, t, :, :].rearrange("p a h -> p (a h)").bitcast(F32), ident[:, :])
                            produced(last)
                        elif name == "mq":
                            if ph[3] == 0:
                                last_read()
                            b = free()
                            for j in range(2):
                                last = mm(b[:, j * S:(j + 1) * S], sel_m[:, 2 * ph[3] + j, :], max_t[s], start=True, stop=True)
                            produced(last)
                        elif name == "ex":
                            a, ch, blk = ph[1:]
                            at = ATT[a]
                            kt, j = blk % at["kt"], blk // at["kt"]
                            np_ = P if at["kt"] == 2 else NK
                            if blk == 0:
                                last_read()
                            for p in range(2):
                                b = free(p)
                                for h in range(2):
                                    last = mm(b[0:np_, h * S:(h + 1) * S], Ks[s][64 * p:64 * p + 64, 2 * j + h, kt * P:kt * P + np_],
                                              Qs[s][64 * p:64 * p + 64, 2 * j + h, :], start=True, stop=True)
                                produced(last)
                            if blk > 0:
                                if a == 2:
                                    c.at("probs_ready", s, 2 * (blocks[s] - 12))
                                else:
                                    c.at("act_read", s, JOBS[n - 1][1])
                                pv(a, ch, blk - 1, blocks[s] - 1)
                            blocks[s] += 1
                        elif name == "pv_last":
                            a, ch = ph[1:]
                            if a == 2:
                                c.at("probs_ready", s, 2 * (blocks[s] - 12))
                            else:
                                c.at("act_read", s, JOBS[n - 1][1])
                            pv(a, ch, 2 * ATT[a]["kt"] - 1, blocks[s] - 1)
                        elif name == "ot":
                            c.take("o_read", s)
                            b = free()
                            for t in range(TT):
                                for j in range(2):
                                    last = tr(b[:, t * 2 * P + j * P:t * 2 * P + (j + 1) * P], att_t[s][:, j, t * P:(t + 1) * P], ident[:, :])
                            produced(last)
                        elif name == "oproj":
                            last_read()
                            b = free()
                            for t in range(TT):
                                last = product(b[:, t * D:(t + 1) * D], feat_cols(t * P, (t + 1) * P), W(WW, ATT[ph[1]]["o"], 0, D), range(KC))
                            produced(last)
                        elif name == "ffn1":
                            if ph[1:] == (0, 0):
                                last_read()
                            b = free()
                            for m in range(2):
                                f = 4 * ph[1] + 2 * ph[2] + m
                                last = product(b[:, m * S:(m + 1) * S], W(WW, FI + f // 2, (f % 2) * P, (f % 2 + 1) * P), feat_cols(0, S), range(KC))
                            produced(last)
                        elif name == "ffn2":
                            h = ph[1]
                            c.take("gelu_lo", s)
                            for t in range(TT):
                                o = obank[s][t][:, 0:D]
                                gg = tuple((lambda k, u=u: u[:, k, t * P:(t + 1) * P]) for u in (Qs[s], Ks[s]))
                                ww = tuple((lambda k, u=u: u[:, k % 2, FO + 2 * h + k // 2, :]) for u in WW)
                                last = product(o, gg, ww, range(4), acc=h == 1, end=h == 1)
                            c.done(last, "o_full", s)
                        elif name == "ffn8":
                            c.take("fp16_ready", s)
                            b = free()
                            for t in range(TT):
                                for k in range(KC):
                                    last = mm(b[:, t * D:(t + 1) * D], fp16f[s][:, k, t * P:(t + 1) * P], w8[:, k, :], start=k == 0, stop=k == KC - 1)
                            produced(last)
                        elif name == "router":
                            last_read()
                            b = free()
                            for t in range(TT):
                                rr = tuple((lambda k, u=u: u[:, k, :]) for u in (wr_hi, wr_lo))
                                last = product(b[:, t * NE:(t + 1) * NE], feat_cols(t * P, (t + 1) * P), rr, range(KC))
                            produced(last)
                        elif name == "w_t":
                            c.take("weights_ready", s)
                            b = free()
                            for t in range(TT):
                                last = tr(b[0:NE, t * P:(t + 1) * P], sc[s][:, 7, t, :], ident[:, :])
                            produced(last)
                        elif name == "b_experts":
                            last_read()
                            b = free()
                            for t in range(TT):
                                last = mm(b[:, t * D:(t + 1) * D], wt[s][:, t * P:(t + 1) * P], b_ex, start=True, stop=True)
                            produced(last)
                        elif name == "expert":
                            t, e = ph[1], ph[2]
                            b = free()
                            ww = tuple((lambda k, u=u: u[:, k, EX + 2 * e:EX + 2 * e + 2, :].rearrange("p b d -> p (b d)")) for u in WW)
                            last = product(b[:, :], feat_cols(t * P, (t + 1) * P), ww, range(KC))
                            produced(last)
                for s in range(STREAMS):
                    c.at("stored", s, 2 * 16)
                c.check(["bank_full"])


def _constants():
    ident = np.eye(P, dtype=np.float32)
    sel = np.zeros((P, 4, NHP, P), np.float32)
    parts = {0: (0, 1), 1: (2,), 2: (0, 2), 3: (1,)}
    for which, rows in parts.items():
        for hp in range(NHP):
            for p in range(2):
                for r in rows:
                    for d in range(HD):
                        sel[(2 * hp + p) * HD + d, which, hp, 64 * p + r * HD + d] = 1.0
    sel_m = np.zeros((2 * HC, NHP, P), np.float32)
    for t in range(2):
        for p in range(2):
            for hp in range(NHP):
                sel_m[t * HC + p * NHP + hp, hp, 64 * p + ROW_MAX + t] = 1.0
    mark = np.zeros((P, 1), np.float32)
    for p in range(2):
        mark[64 * p + ROW_MAX:64 * p + ROW_MAX + 2] = 1.0
    desc = np.ascontiguousarray(np.broadcast_to(np.arange(NE, 0, -1, dtype=np.float32), (P, NE)))
    return ident, sel.reshape(P, -1), sel_m.reshape(2 * HC, -1), mark, desc


def kernel(**inputs):
    import concourse.bacc as _bacc
    from concourse.bass_utils import run_bass_kernel_spmd as _run

    g = {k: np.asarray(v) for k, v in inputs.items()}
    a, l = "L0_xattn_", "L1_xattn_"
    blocks = [g[a + n] for n in ("cq_w", "ck_w", "cv_w", "co_w", "sq_w", "sk_w", "sv_w", "so_w")]
    blocks += [g[l + n] for n in ("Wq", "Wk", "Wv", "Wo")]
    blocks += [g[a + "fi_w"]]
    blocks += [g[a + "fo_w"][D * j:D * (j + 1)] for j in range(F // D)]
    blocks += [g["L1_ffn_W_experts"][e].T for e in range(NE)]
    ident, sel, sel_m, mark, desc = _constants()
    cols = [g[n].reshape(KC, P).T for n in (a + "cq_b", a + "ck_b", a + "cv_b", a + "sq_b", a + "sk_b", a + "sv_b",
                                           l + "bq", l + "bk", l + "bv", a + "co_g", a + "co_be", a + "so_g", a + "so_be")]
    cols += [g[a + "fi_b"].reshape(F // P, P).T, mark]
    rows = [g[n] for n in (a + "co_b", a + "co_g", a + "co_be", a + "so_g", a + "so_be",
                           a + "fo_g", a + "fo_be", "L0_ffn_bias", l + "bo", a + "so_b", a + "fo_b")]
    mask1 = g["mask_SxS2_bk1"]
    mask1_w = np.ascontiguousarray(np.pad(mask1, ((0, 0), (0, MASK_WORDS * 4 - NK)))).view(np.int32)
    mask1_tw = np.ascontiguousarray(mask1.T).view(np.int32)
    arrays = {
        "x": g["x"], "ctx": g["ctx_1024"], "mask0": g["mask_Bx1x1xS2_ff0"].reshape(B, NK),
        "mask1": mask1_w, "mask1_t": mask1_tw, "weights": np.concatenate(blocks, axis=1),
        "w8_t": g["L0_ffn_weight"].T, "cols": np.concatenate(cols, axis=1),
        "rows": np.broadcast_to(np.stack(rows)[None], (P, NROW + 2, D)),
        "router_t": g["L1_ffn_W_router"].T, "router_b": np.broadcast_to(g["L1_ffn_b_router"][None], (P, NE)),
        "b_experts": g["L1_ffn_b_experts"], "identity": ident, "select": sel, "select_max": sel_m, "descending": desc,
    }
    nc = _bacc.Bacc("TRN2", target_bir_lowering=False, num_devices=1)
    feed, args = {}, []
    for name, v in arrays.items():
        v = np.ascontiguousarray(v)
        feed[f"in_{name}"] = v
        args.append(nc.dram_tensor(f"in_{name}", v.shape, mybir.dt.from_np(v.dtype), kind="ExternalInput").ap())
    args.append(nc.dram_tensor("out_0", (B, S, D), F32, kind="ExternalOutput").ap())
    build(nc, *args)
    r = _run(nc, [feed], core_ids=[0])
    return r.results[0]["out_0"]
```

```python
from contextlib import ExitStack

import numpy as np

import concourse.bass as bass
from concourse import mybir

ALU = mybir.AluOpType
ACT = mybir.ActivationFunctionType
AX = mybir.AxisListType
F32 = mybir.dt.float32
F32R = mybir.dt.float32r
FP16 = mybir.dt.float16
FP8 = mybir.dt.float8e4
U8 = mybir.dt.uint8
I32 = mybir.dt.int32

P = 128
B, S, D = 8, 256, 256
NK = 77
NKP = 78
MASK_WORDS = -(-NK // 4)
H, HD = 16, 16
F = 1024
NE = 8
TT = S // P
KC = D // P
HC = H // KC
NHP = HC // 2
STREAMS = 2
ITERS = B // STREAMS
EPS = 1e-5
NEG = -3.0e38
QSCALE = 1.0 / float(np.sqrt(HD))
FP8_MAX = 448.0

ROW_MAX = 3 * HD

CQ, CK, CV, CO, SQ, SK, SV, SO, LQ, LK, LV, LO = range(12)
FI, FO, EX = 12, 16, 20
NB = EX + NE
WEIGHTS_STEP = 2

B_CQ, B_CK, B_CV, B_SQ, B_SK, B_SV, B_LQ, B_LK, B_LV, G_CO, E_CO, G_SO, E_SO = range(0, 26, 2)
B_FI = 26
NCOL = B_FI + F // P

R_COB, R_G1, R_E1, R_G2, R_E2, R_G3, R_E3, R_FFB, R_LOB = range(9)
NROW = 9

ATT = [
    dict(q=CQ, k=CK, v=CV, o=CO, bq=B_CQ, bk=B_CK, bv=B_CV, ctx=True, kt=1),
    dict(q=SQ, k=SK, v=SV, o=SO, bq=B_SQ, bk=B_SK, bv=B_SV, ctx=False, kt=2),
    dict(q=LQ, k=LK, v=LV, o=LO, bq=B_LQ, bk=B_LK, bv=B_LV, ctx=True, kt=1),
]


def attention_phases(a):
    ctx = ATT[a]["ctx"]

    def stack(c):
        return [("ks", a, c, i) for i in range(1 if ctx else 2)] + [("qs", a, c, i) for i in range(2)]

    def maxima(c, first, end):
        return [("mx", a, c, u) for u in range(first, end)]

    def weigh(c):
        return [("mt", a, c)] + [("mq", a, c, i) for i in range(2)] + [("ex", a, c, b) for b in range(2 * ATT[a]["kt"])]

    n = 4 if ctx else HC
    out = [("vproj", a), ("qk", a, 0)] + stack(0) + maxima(0, 0, n) + weigh(0) + [("pv_last", a, 0), ("ot", a, 0)]
    out += [("qk", a, 1)] + stack(1) + maxima(1, 0, n) + weigh(1) + [("pv_last", a, 1), ("ot", a, 1)]
    return out + [("ao_t", a), ("oproj", a)]


def layernorm(*ph):
    return [("stats", ph[0]), ("moments", ph[0]), ph]


SCHEDULE = (
    [("ctx",)] + layernorm("ln_first") + [("z_t", 0)]
    + attention_phases(0)
    + layernorm("ln_res", 1) + [("z_t", 1)]
    + attention_phases(1)
    + layernorm("ln_res", 2) + [("z_t", 2)]
    + [ph for half in range(2) for ph in [("ffn1", half, 0), ("ffn1", half, 1), ("ffn2", half)]]
    + [("ffn_out",)] + layernorm("ln3") + layernorm("ln_x") + [("z_fp8",), ("ffn8",)]
    + layernorm("ln_x") + [("z_t", 0)]
    + attention_phases(2)
    + layernorm("ln_x") + [("z_t", 0), ("router",), ("route",), ("w_t",), ("b_experts",)]
    + [("expert", tt, e) for tt in range(TT) for e in range(NE // 2)]
    + [("store",)]
)


def jobs_of(ph):
    name = ph[0]
    if name == "qs":
        return ["dve"] if ph[1] == 2 else ["act"]
    if name == "ex":
        return (["dve"] if ph[1] == 2 else ["act"]) * 2
    return {
        "ctx": ["dve"], "z_t": ["dve"], "vproj": ["act"], "qk": ["dve"], "ks": ["act"], "mx": ["dve"],
        "mt": ["act"], "ot": ["dve"], "ao_t": ["dve"], "oproj": ["dve"], "mq": ["dve"], "ffn1": ["act"], "z_fp8": ["dve"],
        "ffn8": ["act"], "router": ["dve"], "w_t": ["act"], "b_experts": ["dve"], "expert": ["dve"],
    }.get(name, [])


JOBS = []
FIRST_JOB = {}
for _i, _ph in enumerate(SCHEDULE):
    FIRST_JOB[_i] = len(JOBS)
    for _e in jobs_of(_ph):
        JOBS.append((_e, 1 + sum(1 for x in JOBS if x[0] == _e)))

JOB_OF = {ph: FIRST_JOB[_i] for _i, ph in enumerate(SCHEDULE)}
FIRST_BLOCK = {_i: sum(1 for x in SCHEDULE[:_i] if x[0] == "ex") for _i in range(len(SCHEDULE))}


NPH = len(SCHEDULE)
AHEAD = SCHEDULE.index(("mt", 0, 0))


def in_step(first, end):
    return [(i, s) for i in range(first, end) for s in range(STREAMS)]


PROLOGUE = in_step(0, AHEAD)
BODY = in_step(AHEAD, NPH) + in_step(0, AHEAD)
EPILOGUE = in_step(AHEAD, NPH)

KEEP_UP = {"z_t": 20, "vproj": 1, "ks": 1, "mx": 4, "mt": 5, "mq": 2, "ex": 2, "ot": 2, "ao_t": 3}
NLOADS = NB // WEIGHTS_STEP
WEIGHTS_AT = {}
for _n in range(NLOADS):
    WEIGHTS_AT.setdefault(2 + _n * (AHEAD - 3) // (NLOADS - 1), []).append(_n)

TOTALS = {
    "loaded": 16 * 4,
    "stored": 16,
    "bank_full": len(JOBS),
    "dve_read": sum(1 for x in JOBS if x[0] == "dve"),
    "act_read": sum(1 for x in JOBS if x[0] == "act"),
    "dve_step": None,
    "act_step": None,
    "pool_step": None,
    "hi_ready": None,
    "feat_ready": None,
    "z_ready": None,
    "var_ready": None,
    "rstd_ready": None,
    "resid_ready": None,
    "x_copied": None,
    "negmax_ready": None,
    "pv_done": None,
    "o_full": None,
    "o_read": None,
    "ffn_read": None,
    "probs_ready": None,
    "gelu_hi": None,
    "gelu_lo": None,
    "fp8_ready": None,
    "fp16_ready": None,
    "logits_ready": None,
    "expl_ready": None,
    "weights_ready": None,
}
COUNTS = {
    "dve_step": 114, "act_step": 14, "pool_step": 3, "hi_ready": 15, "feat_ready": 2, "z_ready": 6,
    "var_ready": 7, "rstd_ready": 7, "resid_ready": 3, "x_copied": 1, "negmax_ready": 6,
    "pv_done": 16, "o_full": 2, "o_read": 6, "ffn_read": 1, "probs_ready": 8, "gelu_hi": 2,
    "gelu_lo": 2, "fp8_ready": 1, "fp16_ready": 1, "logits_ready": 1, "expl_ready": 1,
    "weights_ready": 1,
}
TOTALS.update(COUNTS)


class Count:

    def __init__(self, eng, sems, names):
        self.eng, self.sems, self.names = eng, sems, names
        self.begin(0)
        self.sent, self.taken, self.seen = {}, {}, {}

    def begin(self, it):
        self.it, self.ahead = it, [0] * STREAMS

    def enter(self, i, s):
        if i == 0:
            for d in (self.sent, self.taken, self.seen):
                for key in [k for k in d if k[1] == s]:
                    del d[key]

    def leave(self, i, s):
        if i == NPH - 1:
            for name in self.names:
                got = self.sent.get((name, s), 0)
                assert got == TOTALS[name], (name, s, got, TOTALS[name])
            self.ahead[s] = 1

    def batch(self, s):
        return self.it * STREAMS + (self.ahead[s] * STREAMS + s)

    def counted(self, name, s, by=1):
        self.sent[name, s] = self.sent.get((name, s), 0) + by
        return self.sems[name][s]

    def news(self, name, s, k):
        return self.seen.get((name, s), 0) < k

    def at(self, name, s, k):
        self.seen[name, s] = max(k, self.seen.get((name, s), 0))
        return self.it * TOTALS[name] + (self.ahead[s] * TOTALS[name] + k)

    def before(self, name, s, k):
        return self.it * TOTALS[name] + ((self.ahead[s] - 1) * TOTALS[name] + k)

    def take(self, name, s, by=1):
        self.taken[name, s] = self.taken.get((name, s), 0) + by
        return self.at(name, s, self.taken[name, s])

    def own(self, name, s):
        return self.at(name, s, self.sent[name, s])


def build(nc, x, ctx_in, mask0, mask1, mask1_t, weights, w8_t, cols, rows, router_t, router_b, b_experts,
          identity, select, select_max, descending, out):
    ex = ExitStack()
    with ex:
        def sb(name, shape, dt=F32):
            return ex.enter_context(nc.sbuf_tensor(name, shape, dt))

        def both(name, shape, dt=F32):
            return [sb(f"{name}{s}", shape, dt) for s in range(STREAMS)]

        w_hi = sb("w_hi", [P, KC, NB, D], F32R)
        w_lo = sb("w_lo", [P, KC, NB, D], F32R)
        w8 = sb("w8", [P, KC, D], FP16)
        ident = sb("ident", [P, P])
        sel = sb("sel", [P, 4, NHP, P], F32R)
        sel_m = sb("sel_m", [2 * HC, NHP, P], F32R)
        col = sb("col", [P, NCOL + 1])
        row = sb("row", [P, NROW, D])
        wr_hi = sb("wr_hi", [P, KC, NE], F32R)
        wr_lo = sb("wr_lo", [P, KC, NE], F32R)
        rb = sb("rb", [P, NE])
        desc = sb("desc", [P, NE])
        bias_qk = sb("bias_qk", [P, TT, NK])
        low_rows = sb("low_rows", [P, S])
        some_q = sb("some_q", [P, S])
        some_p = sb("some_p", [P, TT])
        half_neg = sb("half_neg", [P, TT])
        X = both("X", [P, TT, D])
        R = both("R", [P, TT, D])
        Z = both("Z", [P, TT, D])
        feat_hi = both("feat_hi", [P, KC, S], F32R)
        feat_lo = both("feat_lo", [P, KC, S], F32R)
        ctx_hi = both("ctx_hi", [P, KC, NKP], F32R)
        ctx_lo = both("ctx_lo", [P, KC, NKP], F32R)
        q_hi = both("q_hi", [P, 2, S], F32R)
        q_lo = both("q_lo", [P, 2, S], F32R)
        Qs = both("Qs", [P, NHP, S], F32R)
        Ks = both("Ks", [P, NHP, S], F32R)
        Vx = both("Vx", [P, TT, H, HD + 1])
        probs = both("probs", [P, 4, 2 * S])
        att_t = both("att_t", [P, 2, S])
        mask_b = both("mask_b", [P, NK])
        mask_c = both("mask_c", [NK, 1])
        stats = both("stats", [P, TT, 6])
        mv = both("mv", [P, TT, 2])
        ve = both("ve", [P, TT])
        rstd = both("rstd", [P, TT])
        mxv = both("mxv", [P, TT, 2, NHP])
        negm = both("negm", [P, TT, 2, 2 * NHP], F32R)
        recip = both("recip", [P, TT, HC])

        bank = [[ex.enter_context(nc.psum_tensor(f"ring{s}{i}", [P, 512], F32)) for i in range(2)] for s in range(STREAMS)]
        obank = [[ex.enter_context(nc.psum_tensor(f"obank{s}{i}", [P, 512], F32)) for i in range(2)] for s in range(STREAMS)]

        sems = {n: [ex.enter_context(nc.semaphore(f"{n}{s}")) for s in range(STREAMS)] for n in TOTALS}
        setup_pool = ex.enter_context(nc.semaphore("setup_pool"))
        c_in = ex.enter_context(nc.semaphore("consts_loaded"))
        w_in = [ex.enter_context(nc.semaphore(f"raw_weights_loaded{i}")) for i in range(2)]
        w_hi_done = ex.enter_context(nc.semaphore("w_hi_done"))
        w_lo_done = ex.enter_context(nc.semaphore("w_lo_done"))
        setup_dve = ex.enter_context(nc.semaphore("setup_dve"))
        setup_act = ex.enter_context(nc.semaphore("setup_act"))
        count_done = ex.enter_context(nc.semaphore("unmasked_keys_counted"))

        bias_kq = low_rows[0:NK, :]
        b_ex = low_rows[96:96 + NE, :]
        max_t = [q_hi[s][0:2 * HC, 0, :] for s in range(STREAMS)]
        sc = [probs[s][:, 1, 0:8 * TT * NE].rearrange("p (n t e) -> p n t e", n=8, t=TT) for s in range(STREAMS)]
        sc1 = [probs[s][:, 1, 8 * TT * NE:8 * TT * NE + 8 * TT].rearrange("p (n t) -> p n t", n=8) for s in range(STREAMS)]
        wt = [probs[s][96:96 + NE, 2, 0:S] for s in range(STREAMS)]
        sm = [att_t[s][:, :, :].rearrange("p a b -> p (a b)")[:, 0:NHP * NK] for s in range(STREAMS)]
        m8_words = R[1][:, 0, 0:TT * MASK_WORDS].bitcast(I32).rearrange("p (t w) -> p t w", t=TT)
        m8 = R[1][:, 0, 0:TT * MASK_WORDS].bitcast(U8).rearrange("p (t k) -> p t k", t=TT)[:, :, 0:NK]
        m8t_words = R[1][0:NK, 1, 0:S // 4].bitcast(I32)
        m8t = R[1][0:NK, 1, 0:S // 4].bitcast(U8)
        sel_raw = [probs[0][:, 2 * i:2 * i + 2, :].rearrange("p a b -> p (a b)") for i in range(2)]
        sel_m_raw = Z[0][0:2 * HC, :, :].rearrange("p a b -> p (a b)")
        router_raw = X[1][:, 0, 0:KC * NE].rearrange("p (k e) -> p k e", k=KC)
        feat = [probs[s][:, 0, :].rearrange("p (c t) -> p c t", c=KC) for s in range(STREAMS)]
        gelu = [probs[s][:, :, :].rearrange("p n (c t) -> p (n c) t", c=2) for s in range(STREAMS)]
        fp8f = [att_t[s][:, 0, 0:128].bitcast(FP8).rearrange("p (c t) -> p c t", c=KC) for s in range(STREAMS)]
        fp16f = [att_t[s][:, 1, :].bitcast(FP16).rearrange("p (c t) -> p c t", c=KC) for s in range(STREAMS)]
        out16 = [att_t[s][:, 0, :].bitcast(FP16).rearrange("p (t d) -> p t d", t=TT) for s in range(STREAMS)]
        raw = [probs[1][:, 2 * i:2 * i + 2, :].rearrange("p n m -> p (n m)").rearrange("p (k n) -> p k n", k=KC)
               for i in range(2)]
        N_CONST = 14
        N_SETUP = 25 + TT

        def row3(j):
            return row[:, j, :].unsqueeze(1).to_broadcast([P, TT, D])

        block = ex.enter_context(nc.Block())

        @block.sync
        def _(eng):
            eng.dma_start(ident[:, :], identity).then_inc(c_in, 16)
            eng.dma_start(m8_words, mask1.rearrange("(t p) w -> p t w", p=P)).then_inc(c_in, 16)
            eng.dma_start(m8t_words, mask1_t).then_inc(c_in, 16)
            eng.dma_start(col[:, :], cols).then_inc(c_in, 16)
            eng.dma_start(rb[:, :], router_b).then_inc(c_in, 16)
            eng.dma_start(desc[:, :], descending).then_inc(c_in, 16)
            eng.dma_start(b_ex, b_experts).then_inc(c_in, 16)
            eng.dma_start(sel_raw[0], select[:, 0:4 * P * 2]).then_inc(c_in, 16)
            eng.dma_start(sel_raw[1], select[:, 4 * P * 2:4 * P * 4]).then_inc(c_in, 16)
            eng.dma_start(sel_m_raw, select_max).then_inc(c_in, 16)
            eng.dma_start(router_raw, router_t.rearrange("(k p) e -> p k e", p=P)).then_inc(c_in, 16)
            eng.dma_start(att_t[0][:, :, :], w8_t.rearrange("(k p) f -> p k f", p=P)).then_inc(c_in, 16)
            eng.dma_start(row[:, :, :], rows[:, 0:NROW, :]).then_inc(c_in, 16)
            eng.dma_start(X[0][:, :, :], rows[:, NROW:NROW + 2, :]).then_inc(c_in, 16)

            def load_weights(n):
                if n >= 2:
                    eng.wait_ge(w_lo_done, n - 1)
                eng.dma_start(raw[n % 2], weights[:, n * WEIGHTS_STEP * D:(n + 1) * WEIGHTS_STEP * D]
                              .rearrange("(k p) n -> p k n", p=P)).then_inc(w_in[n % 2], 16)

            for n in range(2):
                load_weights(n)
            eng.wait_ge(setup_act, 4)
            eng.wait_ge(setup_pool, 9)
            eng.wait_ge(setup_dve, N_SETUP)
            c = Count(eng, sems, ["stored"])

            def load(s, b):
                for dst, src in ((R[s][:, :, :], x[b].rearrange("(t p) d -> p t d", p=P)), (att_t[s][0:NK, 0, :], ctx_in[b]),
                                 (mask_b[s][:, :], mask0[b].partition_broadcast(P)),
                                 (mask_c[s][:, :], mask0[b].rearrange("(k a) -> k a", a=1))):
                    eng.dma_start(dst, src).then_inc(sems["loaded"][s], 16)

            def phases(order, more=True):
                for i, s in order:
                    c.enter(i, s)
                    ph = SCHEDULE[i]
                    if ph == ("oproj", 2) and more:
                        if c.news("dve_read", s, JOBS[FIRST_JOB[i]][1]):
                            eng.wait_ge(sems["dve_read"][s], c.at("dve_read", s, JOBS[FIRST_JOB[i]][1]))
                        load(s, c.batch(s) + STREAMS)
                    elif ph[0] == "store":
                        if c.news("dve_read", s, TOTALS["dve_read"]):
                            eng.wait_ge(sems["dve_read"][s], c.at("dve_read", s, TOTALS["dve_read"]))
                        eng.dma_start(out[c.batch(s)].rearrange("(t p) d -> p t d", p=P), X[s][:, :, :]).then_inc(c.counted("stored", s, 16), 16)
                    c.leave(i, s)

            for s in range(STREAMS):
                load(s, s)
            for n in range(2, NLOADS):
                load_weights(n)
            phases(PROLOGUE)
            with eng.Fori(0, ITERS - 1) as it:
                c.begin(it)
                phases(BODY)
            c.begin(ITERS - 1)
            phases(EPILOGUE, more=False)
            for s in range(STREAMS):
                eng.wait_ge(sems["stored"][s], 16 * (ITERS + 1))

        @block.gpsimd
        def _(eng):
            g = nc.gpsimd
            g.memset(half_neg[:, :], -0.5).then_inc(setup_pool, 1)
            for s in range(STREAMS):
                g.memset(ve[s][:, :], 0.0).then_inc(sems["stored"][s], 16)
            for s in range(STREAMS):
                g.memset(Vx[s][:, :, :, :], 1.0).then_inc(setup_pool, 1)
                g.memset(ctx_hi[s][:, :, :].bitcast(F32), 0.0).then_inc(setup_pool, 1)
                g.memset(ctx_lo[s][:, :, :].bitcast(F32), 0.0).then_inc(setup_pool, 1)
            eng.wait_ge(c_in, 16 * N_CONST)
            g.tensor_tensor(row[:, R_E1, :], row[:, R_E1, :], X[0][:, 0, :], ALU.add).then_inc(setup_pool, 1)
            g.tensor_tensor(row[:, R_E2, :], row[:, R_E2, :], X[0][:, 1, :], ALU.add).then_inc(setup_pool, 1)
            eng.wait_ge(setup_pool, 9)
            c = Count(eng, sems, ["pool_step", "rstd_ready", "resid_ready"])

            def inverse_root(s):
                eng.wait_ge(sems["var_ready"][s], c.take("var_ready", s))
                g.tensor_tensor(rstd[s][:, :], ve[s][:, :], half_neg[:, :], ALU.pow).then_inc(c.counted("rstd_ready", s), 1)

            def phases(order):
                for i, s in order:
                    c.enter(i, s)
                    ph = SCHEDULE[i]
                    if ph[0] in ("ln_first", "ln_res", "ln3", "ln_x"):
                        inverse_root(s)
                    if ph[0] == "ln_first":
                        eng.wait_ge(sems["z_ready"][s], c.take("z_ready", s))
                        eng.wait_ge(sems["x_copied"][s], c.take("x_copied", s))
                        g.tensor_tensor(X[s][:, :, :], X[s][:, :, :], row3(R_E3), ALU.add).then_inc(c.counted("pool_step", s), 1)
                        g.tensor_tensor(R[s][:, :, :], Z[s][:, :, :], row3(R_COB), ALU.add).then_inc(c.counted("resid_ready", s), 1)
                    elif ph[0] == "ln_res":
                        eng.wait_ge(sems["z_ready"][s], c.take("z_ready", s))
                        g.tensor_tensor(R[s][:, :, :], Z[s][:, :, :], row3(R_G1 if ph[1] == 1 else R_G2), ALU.mult).then_inc(c.counted("pool_step", s), 1)
                        eng.wait_ge(sems["pool_step"][s], c.own("pool_step", s))
                        g.tensor_tensor(R[s][:, :, :], R[s][:, :, :], row3(R_E1 if ph[1] == 1 else R_E2), ALU.add).then_inc(c.counted("resid_ready", s), 1)
                    c.leave(i, s)

            phases(PROLOGUE)
            with eng.Fori(0, ITERS - 1) as it:
                c.begin(it)
                phases(BODY)
            c.begin(ITERS - 1)
            phases(EPILOGUE)

        @block.scalar
        def _(eng):
            a_ = nc.scalar
            eng.wait_ge(c_in, 16 * N_CONST)
            a_.activation(sel[:, 0:2, :, :].rearrange("p w h d -> p (w h d)"), sel_raw[0], ACT.Copy).then_inc(setup_act, 1)
            a_.activation(sel[:, 2:4, :, :].rearrange("p w h d -> p (w h d)"), sel_raw[1], ACT.Copy).then_inc(setup_act, 1)
            a_.activation(sel_m[:, :, :].rearrange("p h k -> p (h k)"), sel_m_raw, ACT.Copy).then_inc(setup_act, 1)
            a_.activation(wr_hi[:, :, :], router_raw, ACT.Copy).then_inc(setup_act, 1)
            eng.wait_ge(setup_pool, 9)
            eng.wait_ge(setup_dve, N_SETUP)
            c = Count(eng, sems, ["act_step", "act_read", "x_copied", "hi_ready", "o_read", "probs_ready", "gelu_hi", "fp16_ready", "expl_ready"])

            def split_weights(n):
                eng.wait_ge(w_in[n % 2], 16 * (n // 2 + 1))
                a_.activation(w_hi[:, :, n * WEIGHTS_STEP:(n + 1) * WEIGHTS_STEP, :],
                              raw[n % 2].rearrange("p k (b d) -> p k b d", d=D), ACT.Copy).then_inc(w_hi_done, 1)

            def phases(order, weights_at=()):
                for i, s in order:
                    c.enter(i, s)
                    ph = SCHEDULE[i]
                    name = ph[0]
                    if s == 0 and i in weights_at:
                        for n in weights_at[i]:
                            split_weights(n)
                    n, blk = FIRST_JOB[i], FIRST_BLOCK[i]

                    if name == "ctx":
                        eng.wait_ge(sems["bank_full"][s], c.at("bank_full", s, n + 1))
                        b = bank[s][n % 2]
                        a_.activation(ctx_hi[s][:, :, 0:NK], b[:, 0:2 * NK].rearrange("p (c k) -> p c k", c=KC), ACT.Copy).then_inc(c.counted("hi_ready", s), 1)
                    elif name == "ln_first":
                        eng.wait_ge(sems["loaded"][s], c.take("loaded", s, 64))
                        if c.news("stored", s, 16):
                            eng.wait_ge(sems["stored"][s], c.at("stored", s, 16))
                        a_.activation(X[s][:, :, :], R[s][:, :, :], ACT.Copy).then_inc(c.counted("x_copied", s), 1)
                    elif name == "z_t":
                        if ph[1]:
                            eng.wait_ge(sems["feat_ready"][s], c.take("feat_ready", s))
                            a_.activation(feat_hi[s][:, :, :], feat[s], ACT.Copy).then_inc(c.counted("hi_ready", s), 1)
                        else:
                            eng.wait_ge(sems["bank_full"][s], c.at("bank_full", s, n + 1))
                            b = bank[s][n % 2]
                            a_.activation(feat_hi[s][:, :, :], b[:, :].rearrange("p (c t) -> p c t", c=KC), ACT.Copy).then_inc(c.counted("hi_ready", s), 1)
                    elif name == "vproj":
                        eng.wait_ge(sems["bank_full"][s], c.at("bank_full", s, n + 1))
                        b = bank[s][n % 2]
                        kt = ATT[ph[1]]["kt"]
                        np_ = P if kt == 2 else NK
                        a_.activation(Vx[s][0:np_, 0:kt, :, 0:HD],
                                             b[0:np_, 0:kt * D].rearrange("p (t h d) -> p t h d", t=kt, d=HD), ACT.Copy).then_inc(c.counted("act_read", s), 1)
                    elif name == "qk":
                        eng.wait_ge(sems["bank_full"][s], c.at("bank_full", s, n + 1))
                        b = bank[s][n % 2]
                        at, ch = ATT[ph[1]], ph[2]
                        nk = NKP if at["ctx"] else S
                        a_.activation(q_hi[s][:, 0, :], b[:, 0:S], ACT.Identity, bias=col[:, at["bq"] + ch:at["bq"] + ch + 1]).then_inc(c.counted("act_step", s), 1)
                        a_.activation(q_hi[s][:, 1, 0:nk], b[:, S:S + nk], ACT.Identity, bias=col[:, at["bk"] + ch:at["bk"] + ch + 1]).then_inc(c.counted("hi_ready", s), 1)
                    elif name == "ks":
                        eng.wait_ge(sems["bank_full"][s], c.at("bank_full", s, n + 1))
                        b = bank[s][n % 2]
                        if ATT[ph[1]]["ctx"]:
                            o, v = Ks[s][:, :, 0:NKP], b[:, 0:NHP * NKP].rearrange("p (h k) -> p h k", h=NHP)
                        else:
                            o, v = Ks[s][:, 2 * ph[3]:2 * ph[3] + 2, :], b[:, :].rearrange("p (h k) -> p h k", h=2)
                        a_.activation(o, v, ACT.Identity, bias=col[:, NCOL:NCOL + 1]).then_inc(c.counted("act_read", s), 1)
                    elif name == "qs" and ph[1] != 2:
                        eng.wait_ge(sems["bank_full"][s], c.at("bank_full", s, n + 1))
                        b = bank[s][n % 2]
                        a_.activation(Qs[s][:, 2 * ph[3]:2 * ph[3] + 2, :], b[:, :].rearrange("p (h k) -> p h k", h=2), ACT.Copy).then_inc(c.counted("act_read", s), 1)
                    elif name == "mt":
                        eng.wait_ge(sems["bank_full"][s], c.at("bank_full", s, n + 1))
                        b = bank[s][n % 2]
                        a_.activation(max_t[s], b[0:2 * HC, 0:S], ACT.Copy).then_inc(c.counted("act_read", s), 1)
                    elif name == "ex":
                        at = ATT[ph[1]]
                        np_ = P if at["kt"] == 2 else NK
                        for k in range(2):
                            slot = 2 * (blk % 2) + k
                            if ph[1] == 2:
                                if c.news("dve_read", s, JOBS[n + k][1]):
                                    eng.wait_ge(sems["dve_read"][s], c.at("dve_read", s, JOBS[n + k][1]))
                                src = probs[s][0:np_, slot, :]
                            else:
                                eng.wait_ge(sems["bank_full"][s], c.at("bank_full", s, n + k + 1))
                                src = bank[s][(n + k) % 2][0:np_, :]
                                if blk >= 2 and k == 0:
                                    if c.news("pv_done", s, blk - 1):
                                        eng.wait_ge(sems["pv_done"][s], c.at("pv_done", s, blk - 1))
                            if ph[1] == 0:
                                ins = a_.activation(probs[s][0:np_, slot, :], src, ACT.Exp, scale=QSCALE, bias=mask_c[s][:, :])
                            else:
                                ins = a_.activation(probs[s][0:np_, slot, :], src, ACT.Exp, scale=QSCALE)
                            ins.then_inc(c.counted("probs_ready" if ph[1] == 2 else "act_read", s), 1)
                    elif name == "ot":
                        if c.news("pv_done", s, FIRST_BLOCK[i]):
                            eng.wait_ge(sems["pv_done"][s], c.at("pv_done", s, FIRST_BLOCK[i]))
                        a_.activation(att_t[s][:, :, :], obank[s][ph[2]][:, :].rearrange("p (c t) -> p c t", c=2), ACT.Copy).then_inc(c.counted("o_read", s), 1)
                    elif name == "ao_t":
                        eng.wait_ge(sems["bank_full"][s], c.at("bank_full", s, n + 1))
                        b = bank[s][n % 2]
                        bv = ATT[ph[1]]["bv"]
                        a_.activation(feat_hi[s][:, 0, :], b[:, 0:S], ACT.Identity, bias=col[:, bv:bv + 1]).then_inc(c.counted("act_step", s), 1)
                        a_.activation(feat_hi[s][:, 1, :], b[:, S:2 * S], ACT.Identity, bias=col[:, bv + 1:bv + 2]).then_inc(c.counted("hi_ready", s), 1)
                    elif name == "ffn1":
                        eng.wait_ge(sems["bank_full"][s], c.at("bank_full", s, n + 1))
                        b = bank[s][n % 2]
                        f = 4 * ph[1] + 2 * ph[2]
                        a_.activation(gelu[s][:, f, :], b[:, 0:S], ACT.Gelu, bias=col[:, B_FI + f:B_FI + f + 1]).then_inc(c.counted("act_step", s), 1)
                        a_.activation(gelu[s][:, f + 1, :], b[:, S:2 * S], ACT.Gelu, bias=col[:, B_FI + f + 1:B_FI + f + 2]).then_inc(c.counted("act_read", s), 1)
                        if ph[2] == 1:
                            eng.wait_ge(sems["act_read"][s], c.own("act_read", s))
                            if ph[1]:
                                if c.news("o_full", s, 1):
                                    eng.wait_ge(sems["o_full"][s], c.at("o_full", s, 1))
                            a_.activation(Qs[s][:, :, :], gelu[s][:, 4 * ph[1]:4 * ph[1] + 4, :], ACT.Copy).then_inc(c.counted("gelu_hi", s), 1)
                    elif name == "z_fp8":
                        eng.wait_ge(sems["fp8_ready"][s], c.take("fp8_ready", s))
                        a_.activation(att_t[s][:, 0, S - 1:S], col[:, 0:1], ACT.Copy).then_inc(c.counted("act_step", s), 1)
                        a_.activation(fp16f[s], fp8f[s], ACT.Copy).then_inc(c.counted("fp16_ready", s), 1)
                    elif name == "ffn8":
                        eng.wait_ge(sems["bank_full"][s], c.at("bank_full", s, n + 1))
                        b = bank[s][n % 2]
                        eng.wait_ge(sems["act_step"][s], c.own("act_step", s))
                        a_.activation(out16[s], b[:, :].rearrange("p (t d) -> p t d", t=TT), ACT.Copy).then_inc(c.counted("act_read", s), 1)
                    elif name == "route":
                        eng.wait_ge(sems["logits_ready"][s], c.take("logits_ready", s))
                        a_.activation(sc[s][:, 1, :, :], sc[s][:, 0, :, :], ACT.Exp).then_inc(c.counted("expl_ready", s), 1)
                    elif name == "w_t":
                        eng.wait_ge(sems["bank_full"][s], c.at("bank_full", s, n + 1))
                        b = bank[s][n % 2]
                        a_.activation(wt[s], b[0:NE, 0:S], ACT.Copy).then_inc(c.counted("act_read", s), 1)
                    c.leave(i, s)

            phases(PROLOGUE, WEIGHTS_AT)
            with eng.Fori(0, ITERS - 1) as it:
                c.begin(it)
                phases(BODY)
            c.begin(ITERS - 1)
            phases(EPILOGUE)

        @block.vector
        def _(eng):
            v = nc.vector
            n_set = [0]

            def setup(ins):
                n_set[0] += 1
                ins.then_inc(setup_dve, 1)
                eng.wait_ge(setup_dve, n_set[0])

            for s in range(STREAMS):
                for i in range(2):
                    setup(v.memset(obank[s][i][:, :], 0.0))
            eng.wait_ge(c_in, 16 * N_CONST)
            eng.wait_ge(setup_act, 4)
            eng.wait_ge(setup_pool, 9)
            setup(v.tensor_tensor(wr_lo[:, :, :], router_raw, wr_hi[:, :, :].bitcast(F32), ALU.subtract))
            mag = Z[0][:, :, :]
            small = att_t[1][:, :, :]
            large = Z[1][:, :, :]
            f8 = R[0][:, 1, 0:128].bitcast(FP8).rearrange("p (k f) -> p k f", k=KC)
            raw8 = att_t[0][:, :, :]
            setup(v.tensor_scalar(mag, raw8, 16.0, -16.0, ALU.min, ALU.max))
            setup(v.tensor_copy(f8, mag, saturate=False))
            setup(v.tensor_copy(small, f8))
            setup(v.tensor_scalar(mag, raw8, FP8_MAX, -FP8_MAX, ALU.min, ALU.max))
            setup(v.tensor_scalar(large, mag, 0.5, None, ALU.mult))
            setup(v.tensor_copy(f8, large, saturate=False))
            setup(v.tensor_copy(large, f8))
            setup(v.tensor_scalar(large, large, 2.0, None, ALU.mult))
            setup(v.tensor_tensor(large, large, small, ALU.subtract))
            setup(v.tensor_tensor(mag, mag, mag, ALU.mult))
            setup(v.tensor_scalar(mag, mag, 256.0, None, ALU.is_gt))
            setup(v.tensor_tensor(large, large, mag, ALU.mult))
            setup(v.tensor_tensor(w8[:, :, :], small, large, ALU.add))
            mf = R[0][:, 1, 0:TT * NK].rearrange("p (t k) -> p t k", t=TT)
            mft = R[0][0:NK, 0, :]
            setup(v.tensor_copy(mf, m8))
            setup(v.tensor_copy(mft, m8t))
            setup(v.tensor_reduce(some_p[:, :], mf, AX.X, ALU.max))
            setup(v.tensor_scalar(mf, mf, -NEG, NEG, ALU.mult, ALU.add))
            for t in range(TT):
                setup(v.tensor_scalar(bias_qk[:, t, :], mf[:, t, :], some_p[:, t:t + 1], None, ALU.mult))
            eng.wait_ge(count_done, 1)
            setup(v.tensor_scalar(some_q[:, :], bank[0][0][:, 0:S], 1.0, None, ALU.min))
            setup(v.tensor_scalar(mft, mft, -NEG, NEG, ALU.mult, ALU.add))
            setup(v.tensor_tensor(bias_kq, mft, some_q[0:NK, :], ALU.mult))
            assert n_set[0] == N_SETUP, n_set
            c = Count(eng, sems, ["dve_read", "dve_step", "z_ready", "var_ready", "feat_ready", "negmax_ready", "gelu_lo",
                                  "ffn_read", "fp8_ready", "logits_ready", "weights_ready"])

            def split_weights(n):
                eng.wait_ge(w_hi_done, n + 1)
                v.tensor_tensor(w_lo[:, :, n * WEIGHTS_STEP:(n + 1) * WEIGHTS_STEP, :],
                                raw[n % 2].rearrange("p k (b d) -> p k b d", d=D),
                                w_hi[:, :, n * WEIGHTS_STEP:(n + 1) * WEIGHTS_STEP, :].bitcast(F32),
                                ALU.subtract).then_inc(w_lo_done, 1)

            def normed(s, kind):
                return {"ln_first": R, "ln_x": X, "ln_res": Z, "ln3": Z}[kind][s]

            def normalise(s, src, signal="z_ready"):
                eng.wait_ge(sems["rstd_ready"][s], c.take("rstd_ready", s))
                for t in range(TT):
                    ins = v.tensor_scalar(Z[s][:, t, :], src[:, t, :], mv[s][:, t, 0:1], rstd[s][:, t:t + 1], ALU.subtract, ALU.mult)
                    if t < TT - 1:
                        ins.then_inc(c.counted("dve_step", s), 1)
                    else:
                        ins.then_inc(c.counted(signal, s), 1)

            def low_part(s, o, src, hi, bias=None):
                if bias is None:
                    return v.tensor_tensor(o, src, hi.bitcast(F32), ALU.subtract)
                return v.scalar_tensor_tensor(o, src, bias, hi.bitcast(F32), ALU.add, ALU.subtract)

            def phases(order, weights_at=()):
                for i, s in order:
                    c.enter(i, s)
                    ph = SCHEDULE[i]
                    name = ph[0]
                    n = FIRST_JOB[i]
                    if s == 0 and i in weights_at:
                        for w in weights_at[i]:
                            split_weights(w)

                    if name == "ctx":
                        eng.wait_ge(sems["loaded"][s], c.take("loaded", s, 64))
                        v.tensor_scalar(mask_b[s][:, :], mask_b[s][:, :], 1.0 / QSCALE, NEG, ALU.mult, ALU.max).then_inc(c.counted("dve_step", s), 1)
                        eng.wait_ge(sems["dve_step"][s], c.own("dve_step", s))
                        eng.wait_ge(sems["bank_full"][s], c.at("bank_full", s, n + 1))
                        b = bank[s][n % 2]
                        eng.wait_ge(sems["hi_ready"][s], c.take("hi_ready", s))
                        low_part(s, ctx_lo[s][:, :, 0:NK], b[:, 0:2 * NK].rearrange("p (c k) -> p c k", c=KC), ctx_hi[s][:, :, 0:NK]).then_inc(c.counted("dve_read", s), 1)
                    elif name == "stats":
                        for t in range(TT):
                            v.bn_stats(stats[s][:, t, :], normed(s, ph[1])[:, t, :]).then_inc(c.counted("dve_step", s), 1)
                    elif name == "moments":
                        eng.wait_ge(sems["dve_step"][s], c.own("dve_step", s))
                        v.memset(recip[s][:, 0, 0:1], 0.0).then_inc(c.counted("dve_step", s), 1)
                        for t in range(TT):
                            v.bn_aggr(mv[s][:, t, :], stats[s][:, t, :]).then_inc(c.counted("dve_step", s), 1)
                        eng.wait_ge(sems["dve_step"][s], c.own("dve_step", s))
                        v.tensor_scalar(ve[s][:, :], mv[s][:, :, 1], EPS, None, ALU.add).then_inc(c.counted("var_ready", s), 1)
                    elif name in ("ln_first", "ln_x", "ln_res"):
                        normalise(s, normed(s, name))
                    elif name == "z_t":
                        eng.wait_ge(sems["bank_full"][s], c.at("bank_full", s, n + 1))
                        b = bank[s][n % 2]
                        bv = b[:, :].rearrange("p (c t) -> p c t", c=KC)
                        if ph[1]:
                            g_, e_ = (G_CO, E_CO) if ph[1] == 1 else (G_SO, E_SO)
                            for ch in range(KC):
                                ins = v.tensor_scalar(feat[s][:, ch, :], bv[:, ch, :], col[:, g_ + ch:g_ + ch + 1], col[:, e_ + ch:e_ + ch + 1], ALU.mult, ALU.add)
                                if ch < KC - 1:
                                    ins.then_inc(c.counted("dve_step", s), 1)
                                else:
                                    ins.then_inc(c.counted("feat_ready", s), 1)
                            eng.wait_ge(sems["feat_ready"][s], c.own("feat_ready", s))
                            bv = feat[s]
                        eng.wait_ge(sems["hi_ready"][s], c.take("hi_ready", s))
                        low_part(s, feat_lo[s][:, :, :], bv, feat_hi[s][:, :, :]).then_inc(c.counted("dve_read", s), 1)
                    elif name == "qk":
                        eng.wait_ge(sems["bank_full"][s], c.at("bank_full", s, n + 1))
                        b = bank[s][n % 2]
                        at, ch = ATT[ph[1]], ph[2]
                        nk = NKP if at["ctx"] else S
                        eng.wait_ge(sems["hi_ready"][s], c.take("hi_ready", s))
                        low_part(s, q_lo[s][:, 0, :], b[:, 0:S], q_hi[s][:, 0, :], col[:, at["bq"] + ch:at["bq"] + ch + 1]).then_inc(c.counted("dve_step", s), 1)
                        low_part(s, q_lo[s][:, 1, 0:nk], b[:, S:S + nk], q_hi[s][:, 1, 0:nk], col[:, at["bk"] + ch:at["bk"] + ch + 1]).then_inc(c.counted("dve_read", s), 1)
                    elif name == "qs" and ph[1] == 2:
                        eng.wait_ge(sems["bank_full"][s], c.at("bank_full", s, n + 1))
                        b = bank[s][n % 2]
                        v.tensor_tensor(Qs[s][:, 2 * ph[3]:2 * ph[3] + 2, :], b[:, :].rearrange("p (h k) -> p h k", h=2),
                                               some_q[:, :].unsqueeze(1).to_broadcast([P, 2, S]), ALU.mult).then_inc(c.counted("dve_read", s), 1)
                    elif name == "mx":
                        eng.wait_ge(sems["bank_full"][s], c.at("bank_full", s, n + 1))
                        b = bank[s][n % 2]
                        if ATT[ph[1]]["ctx"]:
                            p, q = ph[3] // TT, ph[3] % TT
                            bias = mask_b[s][:, :] if ph[1] == 0 else bias_qk[:, q, :]
                            smv = sm[s].rearrange("p (h k) -> p h k", h=NHP)
                            if ph[3]:
                                eng.wait_ge(sems["dve_step"][s], c.own("dve_step", s))
                            v.tensor_tensor(smv, b[:, 0:NHP * NKP].rearrange("p (h k) -> p h k", h=NHP)[:, :, 0:NK],
                                                   bias.unsqueeze(1).to_broadcast([P, NHP, NK]), ALU.add).then_inc(c.counted("dve_read", s), 1)
                            eng.wait_ge(sems["dve_read"][s], c.own("dve_read", s))
                            v.tensor_reduce(mxv[s][:, q, p, :], smv, AX.X, ALU.max).then_inc(c.counted("dve_step", s), 1)
                        else:
                            h = ph[3]
                            v.tensor_reduce(mxv[s][:, :, h % 2, h // 2], b[:, :].rearrange("p (t k) -> p t k", t=TT), AX.X, ALU.max).then_inc(c.counted("dve_read", s), 1)
                    elif name == "mt":
                        eng.wait_ge(sems["dve_step" if ATT[ph[1]]["ctx"] else "dve_read"][s], c.own("dve_step" if ATT[ph[1]]["ctx"] else "dve_read", s))
                        mm = mxv[s][:, :, :, :].rearrange("p t a h -> p t (a h)")
                        v.tensor_scalar(negm[s][:, :, 0, :], mm, -1.0, None, ALU.mult).then_inc(c.counted("dve_step", s), 1)
                        eng.wait_ge(sems["dve_step"][s], c.own("dve_step", s))
                        v.scalar_tensor_tensor(negm[s][:, :, 1, :], mm, -1.0, negm[s][:, :, 0, :].bitcast(F32), ALU.mult, ALU.subtract).then_inc(c.counted("negmax_ready", s), 1)
                    elif name == "mq":
                        eng.wait_ge(sems["bank_full"][s], c.at("bank_full", s, n + 1))
                        b = bank[s][n % 2]
                        qv = Qs[s][:, 2 * ph[3]:2 * ph[3] + 2, :]
                        v.tensor_tensor(qv, qv.bitcast(F32), b[:, :].rearrange("p (h k) -> p h k", h=2), ALU.add).then_inc(c.counted("dve_read", s), 1)
                    elif name == "ex" and ph[1] == 2:
                        blk = FIRST_BLOCK[i]
                        for k in range(2):
                            eng.wait_ge(sems["bank_full"][s], c.at("bank_full", s, n + k + 1))
                            b = bank[s][(n + k) % 2]
                            if k == 0:
                                if c.news("pv_done", s, blk - 1):
                                    eng.wait_ge(sems["pv_done"][s], c.at("pv_done", s, blk - 1))
                            v.tensor_tensor(probs[s][0:NK, 2 * (blk % 2) + k, :].rearrange("p (h q) -> p h q", h=2),
                                                   b[0:NK, :].rearrange("p (h q) -> p h q", h=2),
                                                   bias_kq.unsqueeze(1).to_broadcast([NK, 2, S]), ALU.add).then_inc(c.counted("dve_read", s), 1)
                    elif name == "ot":
                        eng.wait_ge(sems["bank_full"][s], c.at("bank_full", s, n + 1))
                        b = bank[s][n % 2]
                        bt = b[:, :].rearrange("p (t g w) -> p t g w", t=TT, w=2 * HD)
                        if ph[2] == 0 and ph[1] < 2:
                            eng.wait_ge(sems["resid_ready"][s], c.take("resid_ready", s))
                        v.reciprocal(recip[s][:, :, :], bt[:, :, :, HD]).then_inc(c.counted("dve_step", s), 1)
                        eng.wait_ge(sems["dve_step"][s], c.own("dve_step", s))
                        v.tensor_tensor(Z[s][:, :, ph[2] * P:(ph[2] + 1) * P].rearrange("p t (g d) -> p t g d", d=HD),
                                               bt[:, :, :, 0:HD], recip[s][:, :, :].unsqueeze(3).to_broadcast([P, TT, HC, HD]), ALU.mult).then_inc(c.counted("dve_read", s), 1)
                    elif name == "ao_t":
                        eng.wait_ge(sems["bank_full"][s], c.at("bank_full", s, n + 1))
                        b = bank[s][n % 2]
                        bv = ATT[ph[1]]["bv"]
                        eng.wait_ge(sems["hi_ready"][s], c.take("hi_ready", s))
                        low_part(s, feat_lo[s][:, 0, :], b[:, 0:S], feat_hi[s][:, 0, :], col[:, bv:bv + 1]).then_inc(c.counted("dve_step", s), 1)
                        low_part(s, feat_lo[s][:, 1, :], b[:, S:2 * S], feat_hi[s][:, 1, :], col[:, bv + 1:bv + 2]).then_inc(c.counted("dve_read", s), 1)
                    elif name == "oproj":
                        eng.wait_ge(sems["bank_full"][s], c.at("bank_full", s, n + 1))
                        b = bank[s][n % 2]
                        bv = b[:, :].rearrange("p (t d) -> p t d", t=TT)
                        if ph[1] < 2:
                            v.tensor_tensor(Z[s][:, :, :], bv, R[s][:, :, :], ALU.add).then_inc(c.counted("dve_read", s), 1)
                            eng.wait_ge(sems["dve_read"][s], c.own("dve_read", s))
                        else:
                            v.tensor_tensor(Z[s][:, :, :], bv, row3(R_LOB), ALU.add).then_inc(c.counted("dve_read", s), 1)
                            eng.wait_ge(sems["dve_read"][s], c.own("dve_read", s))
                            v.tensor_tensor(X[s][:, :, :], X[s][:, :, :], Z[s][:, :, :], ALU.add).then_inc(c.counted("dve_step", s), 1)
                            eng.wait_ge(sems["dve_step"][s], c.own("dve_step", s))
                    elif name == "ffn1" and ph[2] == 1:
                        eng.wait_ge(sems["gelu_hi"][s], c.take("gelu_hi", s))
                        h = ph[1]
                        low_part(s, Ks[s][:, :, :], gelu[s][:, 4 * h:4 * h + 4, :], Qs[s][:, :, :]).then_inc(c.counted("gelu_lo", s), 1)
                    elif name == "ffn_out":
                        eng.wait_ge(sems["resid_ready"][s], c.take("resid_ready", s))
                        if c.news("o_full", s, 2):
                            eng.wait_ge(sems["o_full"][s], c.at("o_full", s, 2))
                        v.tensor_tensor(Z[s][:, 0, :], obank[s][0][:, 0:D], R[s][:, 0, :], ALU.add).then_inc(c.counted("dve_step", s), 1)
                        v.tensor_tensor(Z[s][:, 1, :], obank[s][1][:, 0:D], R[s][:, 1, :], ALU.add).then_inc(c.counted("ffn_read", s), 1)
                        eng.wait_ge(sems["ffn_read"][s], c.own("ffn_read", s))
                    elif name == "ln3":
                        normalise(s, Z[s], "dve_step")
                        eng.wait_ge(sems["dve_step"][s], c.own("dve_step", s))
                        v.tensor_tensor(Z[s][:, :, :], Z[s][:, :, :], row3(R_G3), ALU.mult).then_inc(c.counted("dve_step", s), 1)
                        eng.wait_ge(sems["dve_step"][s], c.own("dve_step", s))
                        v.tensor_tensor(X[s][:, :, :], X[s][:, :, :], Z[s][:, :, :], ALU.add).then_inc(c.counted("dve_step", s), 1)
                        eng.wait_ge(sems["dve_step"][s], c.own("dve_step", s))
                    elif name == "z_fp8":
                        eng.wait_ge(sems["bank_full"][s], c.at("bank_full", s, n + 1))
                        b = bank[s][n % 2]
                        v.tensor_scalar(feat[s], b[:, :].rearrange("p (c t) -> p c t", c=KC), FP8_MAX, -FP8_MAX, ALU.min, ALU.max).then_inc(c.counted("dve_read", s), 1)
                        eng.wait_ge(sems["dve_read"][s], c.own("dve_read", s))
                        v.memset(recip[s][:, 0, 0:1], 0.0).then_inc(c.counted("dve_step", s), 1)
                        v.tensor_copy(fp8f[s], feat[s], saturate=False).then_inc(c.counted("fp8_ready", s), 1)
                    elif name == "ffn8":
                        if c.news("act_read", s, JOBS[n][1]):
                            eng.wait_ge(sems["act_read"][s], c.at("act_read", s, JOBS[n][1]))
                        v.tensor_tensor(Z[s][:, :, :], out16[s], row3(R_FFB), ALU.add).then_inc(c.counted("dve_step", s), 1)
                        eng.wait_ge(sems["dve_step"][s], c.own("dve_step", s))
                        v.tensor_tensor(X[s][:, :, :], X[s][:, :, :], Z[s][:, :, :], ALU.add).then_inc(c.counted("dve_step", s), 1)
                        eng.wait_ge(sems["dve_step"][s], c.own("dve_step", s))
                    elif name == "router":
                        eng.wait_ge(sems["bank_full"][s], c.at("bank_full", s, n + 1))
                        b = bank[s][n % 2]
                        L = sc[s][:, 0, :, :]
                        v.tensor_tensor(L, b[:, 0:TT * NE].rearrange("p (t e) -> p t e", t=TT), rb[:, :].unsqueeze(1).to_broadcast([P, TT, NE]), ALU.add).then_inc(c.counted("dve_read", s), 1)
                        eng.wait_ge(sems["dve_read"][s], c.own("dve_read", s))
                        v.tensor_reduce(sc1[s][:, 0, :], L, AX.X, ALU.max).then_inc(c.counted("dve_step", s), 1)
                        eng.wait_ge(sems["dve_step"][s], c.own("dve_step", s))
                        v.tensor_tensor(L, L, sc1[s][:, 0, :].unsqueeze(2).to_broadcast([P, TT, NE]), ALU.subtract).then_inc(c.counted("logits_ready", s), 1)
                    elif name == "route":
                        def wide(j):
                            return sc1[s][:, j, :].unsqueeze(2).to_broadcast([P, TT, NE])
                        t8 = [sc[s][:, j, :, :] for j in range(8)]
                        E = t8[1]
                        dsc = desc[:, :].unsqueeze(1).to_broadcast([P, TT, NE])
                        eng.wait_ge(sems["expl_ready"][s], c.take("expl_ready", s))
                        v.tensor_reduce(sc1[s][:, 1, :], E, AX.X, ALU.add).then_inc(c.counted("dve_step", s), 1)
                        v.tensor_reduce(sc1[s][:, 2, :], E, AX.X, ALU.max).then_inc(c.counted("dve_step", s), 1)
                        eng.wait_ge(sems["dve_step"][s], c.own("dve_step", s))
                        v.reciprocal(sc1[s][:, 6, :], sc1[s][:, 1, :]).then_inc(c.counted("dve_step", s), 1)
                        v.tensor_tensor(t8[2], E, wide(2), ALU.is_equal).then_inc(c.counted("dve_step", s), 1)
                        eng.wait_ge(sems["dve_step"][s], c.own("dve_step", s))
                        v.tensor_tensor(t8[2], t8[2], dsc, ALU.mult).then_inc(c.counted("dve_step", s), 1)
                        eng.wait_ge(sems["dve_step"][s], c.own("dve_step", s))
                        v.tensor_reduce(sc1[s][:, 3, :], t8[2], AX.X, ALU.max).then_inc(c.counted("dve_step", s), 1)
                        eng.wait_ge(sems["dve_step"][s], c.own("dve_step", s))
                        v.tensor_tensor(t8[3], t8[2], wide(3), ALU.is_equal).then_inc(c.counted("dve_step", s), 1)
                        eng.wait_ge(sems["dve_step"][s], c.own("dve_step", s))
                        v.scalar_tensor_tensor(t8[4], t8[3], -2.0, E, ALU.mult, ALU.add).then_inc(c.counted("dve_step", s), 1)
                        eng.wait_ge(sems["dve_step"][s], c.own("dve_step", s))
                        v.tensor_reduce(sc1[s][:, 4, :], t8[4], AX.X, ALU.max).then_inc(c.counted("dve_step", s), 1)
                        eng.wait_ge(sems["dve_step"][s], c.own("dve_step", s))
                        v.tensor_tensor(t8[5], t8[4], wide(4), ALU.is_equal).then_inc(c.counted("dve_step", s), 1)
                        eng.wait_ge(sems["dve_step"][s], c.own("dve_step", s))
                        v.tensor_tensor(t8[5], t8[5], dsc, ALU.mult).then_inc(c.counted("dve_step", s), 1)
                        eng.wait_ge(sems["dve_step"][s], c.own("dve_step", s))
                        v.tensor_reduce(sc1[s][:, 5, :], t8[5], AX.X, ALU.max).then_inc(c.counted("dve_step", s), 1)
                        eng.wait_ge(sems["dve_step"][s], c.own("dve_step", s))
                        v.tensor_tensor(t8[6], t8[5], wide(5), ALU.is_equal).then_inc(c.counted("dve_step", s), 1)
                        eng.wait_ge(sems["dve_step"][s], c.own("dve_step", s))
                        v.tensor_tensor(t8[6], t8[6], t8[3], ALU.add).then_inc(c.counted("dve_step", s), 1)
                        eng.wait_ge(sems["dve_step"][s], c.own("dve_step", s))
                        v.tensor_tensor(t8[6], t8[6], E, ALU.mult).then_inc(c.counted("dve_step", s), 1)
                        eng.wait_ge(sems["dve_step"][s], c.own("dve_step", s))
                        v.tensor_tensor(t8[7], t8[6], wide(6), ALU.mult).then_inc(c.counted("weights_ready", s), 1)
                        eng.wait_ge(sems["weights_ready"][s], c.own("weights_ready", s))
                    elif name == "b_experts":
                        eng.wait_ge(sems["bank_full"][s], c.at("bank_full", s, n + 1))
                        b = bank[s][n % 2]
                        v.tensor_tensor(X[s][:, :, :], X[s][:, :, :], b[:, :].rearrange("p (t d) -> p t d", t=TT), ALU.add).then_inc(c.counted("dve_read", s), 1)
                        eng.wait_ge(sems["dve_read"][s], c.own("dve_read", s))
                    elif name == "expert":
                        eng.wait_ge(sems["bank_full"][s], c.at("bank_full", s, n + 1))
                        b = bank[s][n % 2]
                        t, e = ph[1], 2 * ph[2]
                        v.scalar_tensor_tensor(X[s][:, t, :], b[:, 0:D], sc[s][:, 7, t, e:e + 1], X[s][:, t, :], ALU.mult, ALU.add).then_inc(c.counted("dve_step", s), 1)
                        eng.wait_ge(sems["dve_step"][s], c.own("dve_step", s))
                        v.scalar_tensor_tensor(X[s][:, t, :], b[:, D:2 * D], sc[s][:, 7, t, e + 1:e + 2], X[s][:, t, :], ALU.mult, ALU.add).then_inc(c.counted("dve_read", s), 1)
                        eng.wait_ge(sems["dve_read"][s], c.own("dve_read", s))
                    c.leave(i, s)

            phases(PROLOGUE, WEIGHTS_AT)
            with eng.Fori(0, ITERS - 1) as it:
                c.begin(it)
                phases(BODY)
            c.begin(ITERS - 1)
            phases(EPILOGUE)

        @block.tensor
        def _(eng):
            mm, tr = nc.tensor.matmul, nc.tensor.transpose
            eng.wait_ge(setup_dve, 20)
            eng.wait_ge(setup_pool, 9)
            all_ones = Vx[0][0:NK, 0, 0:8, :].rearrange("p h d -> p (h d)")[:, 0:P]
            mm(bank[0][0][:, 0:S], all_ones[:, :], R[0][0:NK, 0, :], start=True, stop=True).then_inc(count_done, 1)
            eng.wait_ge(setup_act, 4)
            eng.wait_ge(setup_dve, N_SETUP)
            c = Count(eng, sems, ["bank_full", "pv_done", "o_full"])

            def product(o, left, right, ws, acc=False, end=True):
                (lh, ll), (rh, rl) = left, right
                n = len(ws)
                last = None
                for j, k in enumerate(ws):
                    for m, (l, r) in enumerate(((ll, rh), (lh, rl), (lh, rh))):
                        last = mm(o, l(k), r(k), start=(not acc and j == 0 and m == 0), stop=(end and j == n - 1 and m == 2))
                return last

            def W(which, w, a, b):
                return tuple((lambda k, t=t: t[:, k, w, a:b]) for t in which)

            WW = (w_hi, w_lo)

            def phases(order, weights_at=()):
                for i, s in order:
                    c.enter(i, s)
                    ph = SCHEDULE[i]
                    name = ph[0]
                    if s == 0 and i in weights_at:
                        eng.wait_ge(w_lo_done, weights_at[i][-1] + 1)
                    n, fb = FIRST_JOB[i], FIRST_BLOCK[i]
                    FF = (feat_hi[s], feat_lo[s])
                    CC = (ctx_hi[s], ctx_lo[s])

                    def feat_cols(a, b, t=FF):
                        return tuple((lambda k, u=u: u[:, k, a:b]) for u in t)

                    def free(k=0):
                        j = n + k
                        e, cnt = JOBS[j - 2]
                        if j >= 2:
                            if c.news(f"{e}_read", s, cnt):
                                eng.wait_ge(sems[f"{e}_read"][s], c.at(f"{e}_read", s, cnt))
                        elif c.ahead[s]:
                            eng.wait_ge(sems[f"{e}_read"][s], c.before(f"{e}_read", s, cnt))
                        return bank[s][j % 2]

                    def last_read():
                        e, cnt = JOBS[n - 1]
                        if c.news(f"{e}_read", s, cnt):
                            eng.wait_ge(sems[f"{e}_read"][s], c.at(f"{e}_read", s, cnt))

                    def read_out(*ph, k=0):
                        e, cnt = JOBS[JOB_OF[ph] + k]
                        if c.news(f"{e}_read", s, cnt):
                            eng.wait_ge(sems[f"{e}_read"][s], c.at(f"{e}_read", s, cnt))

                    def features_split():
                        e, cnt = JOBS[FIRST_JOB[max(j for j in range(i) if SCHEDULE[j][0] == "z_t")]]
                        if c.news(f"{e}_read", s, cnt):
                            eng.wait_ge(sems[f"{e}_read"][s], c.at(f"{e}_read", s, cnt))

                    def pv(a, ch, blk, gb):
                        at = ATT[a]
                        kt, j = blk % at["kt"], blk // at["kt"]
                        np_ = P if at["kt"] == 2 else NK
                        for g in range(4):
                            head = ch * HC + 4 * j + g
                            src = probs[s][0:np_, 2 * (gb % 2) + g % 2, (g // 2) * S:(g // 2 + 1) * S]
                            last = mm(obank[s][ch][32 * g:32 * g + HD + 1, j * S:(j + 1) * S], Vx[s][0:np_, kt, head, :], src,
                                      start=(kt == 0), stop=(kt == at["kt"] - 1), tile_position=(0, 32 * g), skip_group_check=True)
                        last.then_inc(c.counted("pv_done", s), 1)

                    for _ in range(KEEP_UP.get(name, 0)):
                        mm(free()[:, 0:D], w_hi[:, 0, 0, 0:P], w_hi[:, 0, 1, :], start=True, stop=True)
                    if name == "ctx":
                        eng.wait_ge(sems["loaded"][s], c.take("loaded", s, 64))
                        b = free()
                        for k in range(KC):
                            last = tr(b[:, k * NK:(k + 1) * NK], att_t[s][0:NK, 0, k * P:(k + 1) * P], ident[0:NK, 0:NK])
                        last.then_inc(c.counted("bank_full", s), 1)
                    elif name in ("z_t", "z_fp8", "ao_t"):
                        if name == "ao_t":
                            last_read()
                        else:
                            eng.wait_ge(sems["z_ready"][s], c.take("z_ready", s))
                        b = free()
                        for k in range(KC):
                            for t in range(TT):
                                last = tr(b[:, k * S + t * P:k * S + (t + 1) * P], Z[s][:, t, k * P:(k + 1) * P], ident[:, :])
                        last.then_inc(c.counted("bank_full", s), 1)
                    elif name == "vproj":
                        at = ATT[ph[1]]
                        features_split()
                        b = free()
                        for t in range(at["kt"]):
                            if at["ctx"]:
                                last = product(b[0:NK, 0:D], feat_cols(0, NK, CC), W(WW, at["v"], 0, D), range(KC))
                            else:
                                last = product(b[:, t * D:(t + 1) * D], feat_cols(t * P, (t + 1) * P), W(WW, at["v"], 0, D), range(KC))
                        last.then_inc(c.counted("bank_full", s), 1)
                    elif name == "qk":
                        at, ch = ATT[ph[1]], ph[2]
                        features_split()
                        b = free()
                        product(b[:, 0:S], W(WW, at["q"], ch * P, (ch + 1) * P), feat_cols(0, S), range(KC))
                        if at["ctx"]:
                            last = product(b[:, S:S + NKP], W(WW, at["k"], ch * P, (ch + 1) * P), feat_cols(0, NKP, CC), range(KC))
                        else:
                            last = product(b[:, S:2 * S], W(WW, at["k"], ch * P, (ch + 1) * P), feat_cols(0, S), range(KC))
                        last.then_inc(c.counted("bank_full", s), 1)
                    elif name in ("ks", "qs"):
                        key = name == "ks"
                        if key and ph[3] == 0:
                            read_out("qk", ph[1], ph[2])
                        b = free()
                        wide = NKP if key and ATT[ph[1]]["ctx"] else S
                        hps = range(NHP) if wide == NKP else (2 * ph[3], 2 * ph[3] + 1)
                        for j, hp in enumerate(hps):
                            o = b[:, j * wide:(j + 1) * wide]
                            mm(o, sel[:, 2 * key, hp, :], q_hi[s][:, int(key), 0:wide], start=True, stop=False)
                            last = mm(o, sel[:, 2 * key + 1, hp, :], q_lo[s][:, int(key), 0:wide], start=False, stop=True)
                        last.then_inc(c.counted("bank_full", s), 1)
                    elif name == "mx":
                        if ph[3] == 0:
                            read_out("ks", ph[1], ph[2], 0 if ATT[ph[1]]["ctx"] else 1)
                            for i_ in range(2):
                                read_out("qs", ph[1], ph[2], i_)
                        b = free()
                        if ATT[ph[1]]["ctx"]:
                            p, q = ph[3] // TT, ph[3] % TT
                            for hp in range(NHP):
                                last = mm(b[:, hp * NKP:(hp + 1) * NKP], Qs[s][64 * p:64 * p + 64, hp, q * P:(q + 1) * P],
                                          Ks[s][64 * p:64 * p + 64, hp, 0:NKP], start=True, stop=True)
                        else:
                            p, hp = ph[3] % 2, ph[3] // 2
                            for q in range(TT):
                                last = mm(b[:, q * S:(q + 1) * S], Qs[s][64 * p:64 * p + 64, hp, q * P:(q + 1) * P],
                                          Ks[s][64 * p:64 * p + 64, hp, :], start=True, stop=True)
                        last.then_inc(c.counted("bank_full", s), 1)
                    elif name == "mt":
                        eng.wait_ge(sems["negmax_ready"][s], c.take("negmax_ready", s))
                        b = free()
                        for t in range(TT):
                            last = tr(b[0:2 * HC, t * P:(t + 1) * P], negm[s][:, t, :, :].rearrange("p a h -> p (a h)").bitcast(F32), ident[:, :])
                        last.then_inc(c.counted("bank_full", s), 1)
                    elif name == "mq":
                        if ph[3] == 0:
                            last_read()
                        b = free()
                        for j in range(2):
                            last = mm(b[:, j * S:(j + 1) * S], sel_m[:, 2 * ph[3] + j, :], max_t[s], start=True, stop=True)
                        last.then_inc(c.counted("bank_full", s), 1)
                    elif name == "ex":
                        a, ch, blk = ph[1:]
                        at = ATT[a]
                        kt, j = blk % at["kt"], blk // at["kt"]
                        np_ = P if at["kt"] == 2 else NK
                        if blk == 0:
                            last_read()
                        for p in range(2):
                            b = free(p)
                            for h in range(2):
                                last = mm(b[0:np_, h * S:(h + 1) * S], Ks[s][64 * p:64 * p + 64, 2 * j + h, kt * P:kt * P + np_],
                                          Qs[s][64 * p:64 * p + 64, 2 * j + h, :], start=True, stop=True)
                            last.then_inc(c.counted("bank_full", s), 1)
                        if blk > 0:
                            if a == 2:
                                if c.news("probs_ready", s, 2 * (fb - 12)):
                                    eng.wait_ge(sems["probs_ready"][s], c.at("probs_ready", s, 2 * (fb - 12)))
                            else:
                                if c.news("act_read", s, JOBS[n - 1][1]):
                                    eng.wait_ge(sems["act_read"][s], c.at("act_read", s, JOBS[n - 1][1]))
                            pv(a, ch, blk - 1, fb - 1)
                    elif name == "pv_last":
                        a, ch = ph[1:]
                        if a == 2:
                            if c.news("probs_ready", s, 2 * (fb - 12)):
                                eng.wait_ge(sems["probs_ready"][s], c.at("probs_ready", s, 2 * (fb - 12)))
                        else:
                            read_out("ex", a, ch, 2 * ATT[a]["kt"] - 1, k=1)
                        pv(a, ch, 2 * ATT[a]["kt"] - 1, fb - 1)
                    elif name == "ot":
                        eng.wait_ge(sems["o_read"][s], c.take("o_read", s))
                        b = free()
                        for t in range(TT):
                            for j in range(2):
                                last = tr(b[:, t * 2 * P + j * P:t * 2 * P + (j + 1) * P], att_t[s][:, j, t * P:(t + 1) * P], ident[:, :])
                        last.then_inc(c.counted("bank_full", s), 1)
                    elif name == "oproj":
                        last_read()
                        b = free()
                        for t in range(TT):
                            last = product(b[:, t * D:(t + 1) * D], feat_cols(t * P, (t + 1) * P), W(WW, ATT[ph[1]]["o"], 0, D), range(KC))
                        last.then_inc(c.counted("bank_full", s), 1)
                    elif name == "ffn1":
                        if ph[1:] == (0, 0):
                            last_read()
                        b = free()
                        for m in range(2):
                            f = 4 * ph[1] + 2 * ph[2] + m
                            last = product(b[:, m * S:(m + 1) * S], W(WW, FI + f // 2, (f % 2) * P, (f % 2 + 1) * P), feat_cols(0, S), range(KC))
                        last.then_inc(c.counted("bank_full", s), 1)
                    elif name == "ffn2":
                        h = ph[1]
                        eng.wait_ge(sems["gelu_lo"][s], c.take("gelu_lo", s))
                        for t in range(TT):
                            o = obank[s][t][:, 0:D]
                            gg = tuple((lambda k, u=u: u[:, k, t * P:(t + 1) * P]) for u in (Qs[s], Ks[s]))
                            ww = tuple((lambda k, u=u: u[:, k % 2, FO + 2 * h + k // 2, :]) for u in WW)
                            last = product(o, gg, ww, range(4), acc=h == 1, end=h == 1)
                        last.then_inc(c.counted("o_full", s), 1)
                    elif name == "ffn8":
                        eng.wait_ge(sems["fp16_ready"][s], c.take("fp16_ready", s))
                        b = free()
                        for t in range(TT):
                            for k in range(KC):
                                last = mm(b[:, t * D:(t + 1) * D], fp16f[s][:, k, t * P:(t + 1) * P], w8[:, k, :], start=k == 0, stop=k == KC - 1)
                        last.then_inc(c.counted("bank_full", s), 1)
                    elif name == "router":
                        last_read()
                        b = free()
                        for t in range(TT):
                            rr = tuple((lambda k, u=u: u[:, k, :]) for u in (wr_hi, wr_lo))
                            last = product(b[:, t * NE:(t + 1) * NE], feat_cols(t * P, (t + 1) * P), rr, range(KC))
                        last.then_inc(c.counted("bank_full", s), 1)
                    elif name == "w_t":
                        eng.wait_ge(sems["weights_ready"][s], c.take("weights_ready", s))
                        b = free()
                        for t in range(TT):
                            last = tr(b[0:NE, t * P:(t + 1) * P], sc[s][:, 7, t, :], ident[:, :])
                        last.then_inc(c.counted("bank_full", s), 1)
                    elif name == "b_experts":
                        last_read()
                        b = free()
                        for t in range(TT):
                            last = mm(b[:, t * D:(t + 1) * D], wt[s][:, t * P:(t + 1) * P], b_ex, start=True, stop=True)
                        last.then_inc(c.counted("bank_full", s), 1)
                    elif name == "expert":
                        t, e = ph[1], ph[2]
                        b = free()
                        ww = tuple((lambda k, u=u: u[:, k, EX + 2 * e:EX + 2 * e + 2, :].rearrange("p b d -> p (b d)")) for u in WW)
                        last = product(b[:, :], feat_cols(t * P, (t + 1) * P), ww, range(KC))
                        last.then_inc(c.counted("bank_full", s), 1)
                    c.leave(i, s)

            phases(PROLOGUE, WEIGHTS_AT)
            with eng.Fori(0, ITERS - 1) as it:
                c.begin(it)
                phases(BODY)
            c.begin(ITERS - 1)
            phases(EPILOGUE)


def _constants():
    ident = np.eye(P, dtype=np.float32)
    sel = np.zeros((P, 4, NHP, P), np.float32)
    parts = {0: (0, 1), 1: (2,), 2: (0, 2), 3: (1,)}
    for which, rows in parts.items():
        for hp in range(NHP):
            for p in range(2):
                for r in rows:
                    for d in range(HD):
                        sel[(2 * hp + p) * HD + d, which, hp, 64 * p + r * HD + d] = 1.0
    sel_m = np.zeros((2 * HC, NHP, P), np.float32)
    for t in range(2):
        for p in range(2):
            for hp in range(NHP):
                sel_m[t * HC + p * NHP + hp, hp, 64 * p + ROW_MAX + t] = 1.0
    mark = np.zeros((P, 1), np.float32)
    for p in range(2):
        mark[64 * p + ROW_MAX:64 * p + ROW_MAX + 2] = 1.0
    desc = np.ascontiguousarray(np.broadcast_to(np.arange(NE, 0, -1, dtype=np.float32), (P, NE)))
    return ident, sel.reshape(P, -1), sel_m.reshape(2 * HC, -1), mark, desc


def kernel(**inputs):
    import concourse.bacc as _bacc
    from concourse.bass_utils import run_bass_kernel_spmd as _run

    g = {k: np.asarray(v) for k, v in inputs.items()}
    a, l = "L0_xattn_", "L1_xattn_"
    blocks = [g[a + n] for n in ("cq_w", "ck_w", "cv_w", "co_w", "sq_w", "sk_w", "sv_w", "so_w")]
    blocks += [g[l + n] for n in ("Wq", "Wk", "Wv", "Wo")]
    blocks += [g[a + "fi_w"]]
    blocks += [g[a + "fo_w"][D * j:D * (j + 1)] for j in range(F // D)]
    blocks += [g["L1_ffn_W_experts"][e].T for e in range(NE)]
    ident, sel, sel_m, mark, desc = _constants()
    cols = [g[n].reshape(KC, P).T for n in (a + "cq_b", a + "ck_b", a + "cv_b", a + "sq_b", a + "sk_b", a + "sv_b",
                                           l + "bq", l + "bk", l + "bv", a + "co_g", a + "co_be", a + "so_g", a + "so_be")]
    cols += [g[a + "fi_b"].reshape(F // P, P).T, mark]
    rows = [g[n] for n in (a + "co_b", a + "co_g", a + "co_be", a + "so_g", a + "so_be",
                           a + "fo_g", a + "fo_be", "L0_ffn_bias", l + "bo", a + "so_b", a + "fo_b")]
    mask1 = g["mask_SxS2_bk1"]
    mask1_w = np.ascontiguousarray(np.pad(mask1, ((0, 0), (0, MASK_WORDS * 4 - NK)))).view(np.int32)
    mask1_tw = np.ascontiguousarray(mask1.T).view(np.int32)
    arrays = {
        "x": g["x"], "ctx": g["ctx_1024"], "mask0": g["mask_Bx1x1xS2_ff0"].reshape(B, NK),
        "mask1": mask1_w, "mask1_t": mask1_tw, "weights": np.concatenate(blocks, axis=1),
        "w8_t": g["L0_ffn_weight"].T, "cols": np.concatenate(cols, axis=1),
        "rows": np.broadcast_to(np.stack(rows)[None], (P, NROW + 2, D)),
        "router_t": g["L1_ffn_W_router"].T, "router_b": np.broadcast_to(g["L1_ffn_b_router"][None], (P, NE)),
        "b_experts": g["L1_ffn_b_experts"], "identity": ident, "select": sel, "select_max": sel_m, "descending": desc,
    }
    nc = _bacc.Bacc("TRN2", target_bir_lowering=False, num_devices=1)
    feed, args = {}, []
    for name, v in arrays.items():
        v = np.ascontiguousarray(v)
        feed[f"in_{name}"] = v
        args.append(nc.dram_tensor(f"in_{name}", v.shape, mybir.dt.from_np(v.dtype), kind="ExternalInput").ap())
    args.append(nc.dram_tensor("out_0", (B, S, D), F32, kind="ExternalOutput").ap())
    build(nc, *args)
    r = _run(nc, [feed], core_ids=[0])
    return r.results[0]["out_0"]
```
